# Optimizing a Trainium2 kernel written in Bass

```python
import numpy as np
import jax
import jax.numpy as jnp

def _softmax(x, axis=-1):
    return jax.nn.softmax(x, axis=axis)

def _gelu(x):
    return jax.nn.gelu(x, approximate=True)

def _silu(x):
    return jax.nn.silu(x)

def _sigmoid(x):
    return jax.nn.sigmoid(x)

def _layernorm(x, axis=-1, eps=1e-05):
    m = jnp.mean(x, axis=axis, keepdims=True)
    v = jnp.var(x, axis=axis, keepdims=True)
    return (x - m) / jnp.sqrt(v + eps)

def _scatter_add(tgt, idx, src, axis=0):
    return tgt.at[idx].add(src)

def _segment_sum(src, seg, n):
    return jax.ops.segment_sum(src, seg, n)
kernel_name = 'mk_macaron_d1_jaxref_r8_cc85b3'

def setup_inputs(seed: int=0):
    np.random.seed(seed)
    _w = jnp.asarray

    def _L0_attn_setup():
        import jax, jax.numpy as jnp
        import numpy as np
        CHUNK = 32
        EPS_L2 = 1e-06
        EPS_RMS = 1e-05
        NUM_HEADS = 4

        def _causal_dwconv_silu(x, w):
            k = w.shape[1]
            l = x.shape[1]
            xp = jnp.pad(x, ((0, 0), (k - 1, 0), (0, 0)))
            out = sum((w[:, j] * xp[:, j:j + l, :] for j in range(k)))
            return jax.nn.silu(out)

        def _l2norm(x):
            return x * jax.lax.rsqrt(jnp.sum(x * x, -1, keepdims=True) + EPS_L2)

        def _delta_rule_chunkwise(q, k, v, beta, c=CHUNK):
            b, h, l, dk = q.shape
            dv = v.shape[-1]
            n = l // c
            q = _l2norm(q)
            k = _l2norm(k)
            v = v * beta[..., None]
            kb = k * beta[..., None]
            qc = q.reshape(b, h, n, c, dk)
            kc = k.reshape(b, h, n, c, dk)
            vc = v.reshape(b, h, n, c, dv)
            kbc = kb.reshape(b, h, n, c, dk)
            strict_lower = jnp.tril(jnp.ones((c, c), bool), -1)
            attn = -jnp.einsum('bhnik,bhnjk->bhnij', kbc, kc)
            attn = jnp.where(strict_lower, attn, 0.0)
            for i in range(1, c):
                upd = jnp.einsum('bhnj,bhnjm->bhnm', attn[..., i, :], attn[..., :, :i])
                attn = attn.at[..., i, :i].add(upd)
            attn = attn + jnp.eye(c, dtype=attn.dtype)
            u = attn @ vc
            w = attn @ kbc
            incl_lower = jnp.tril(jnp.ones((c, c), bool))

            def step(S, inp):
                q_i, k_i, u_i, w_i = inp
                a = jnp.where(incl_lower, jnp.einsum('bhik,bhjk->bhij', q_i, k_i), 0.0)
                u_new = u_i - w_i @ S
                o_i = q_i @ S + a @ u_new
                S = S + jnp.einsum('bhck,bhcv->bhkv', k_i, u_new)
                return (S, o_i)
            S0 = jnp.zeros((b, h, dk, dv), q.dtype)
            xs = tuple((jnp.moveaxis(x, 2, 0) for x in (qc, kc, u, w)))
            S, o = jax.lax.scan(step, S0, xs)
            o = jnp.moveaxis(o, 0, 2).reshape(b, h, l, dv)
            return (o, S)

        def _ema(v, gamma):
            vt = jnp.moveaxis(v, 2, 0)
            gt = jnp.moveaxis(gamma, 2, 0)[..., None]

            def step(s, xg):
                x, g = xg
                s = g * s + (1.0 - g) * x
                return (s, s)
            s0 = jnp.zeros(v.shape[:2] + v.shape[-1:], v.dtype)
            _, out = jax.lax.scan(step, s0, (vt, gt))
            return jnp.moveaxis(out, 0, 2)

        def _forward(hs, Wq, Wk, Wv, Wb, Wdec, Wmix, mix_bias, wq_conv, wk_conv, wv_conv, onorm_w, Wo):
            b, l, d = hs.shape
            h = NUM_HEADS
            q = _causal_dwconv_silu(hs @ Wq.T, wq_conv)
            k = _causal_dwconv_silu(hs @ Wk.T, wk_conv)
            v = _causal_dwconv_silu(hs @ Wv.T, wv_conv)
            dk = q.shape[-1] // h
            dv = v.shape[-1] // h
            q = q.reshape(b, l, h, dk)
            k = k.reshape(b, l, h, dk)
            v = v.reshape(b, l, h, dv)
            beta = jax.nn.sigmoid(hs @ Wb.T)
            qd = jnp.transpose(q, (0, 2, 1, 3))
            kd = jnp.transpose(k, (0, 2, 1, 3))
            vd = jnp.transpose(v, (0, 2, 1, 3))
            bd = jnp.transpose(beta, (0, 2, 1))
            o_d, _S = _delta_rule_chunkwise(qd, kd, vd, bd)
            o_d = jnp.transpose(o_d, (0, 2, 1, 3))
            gamma = jnp.transpose(jax.nn.sigmoid(hs @ Wdec.T), (0, 2, 1))
            ema_out = jnp.transpose(_ema(vd, gamma), (0, 2, 1, 3))
            mix = jax.nn.sigmoid(hs @ Wmix.T + mix_bias)[..., None]
            o = (1.0 - mix) * o_d + mix * ema_out
            o = o * jax.lax.rsqrt(jnp.mean(o * o, -1, keepdims=True) + EPS_RMS) * onorm_w
            return o.reshape(b, l, h * dv) @ Wo.T
        key = jax.random.key(seed)
        ks = jax.random.split(key, 12)
        B, L, D, H, K = (2, 512, 128, 4, 4)
        s = 0.02
        f = jnp.float32
        return {'hidden_states': jax.random.normal(ks[0], (B, L, D), f), 'Wq': jax.random.normal(ks[1], (D, D), f) * s, 'Wk': jax.random.normal(ks[2], (D, D), f) * s, 'Wv': jax.random.normal(ks[3], (D, D), f) * s, 'Wb': jax.random.normal(ks[4], (H, D), f) * s, 'Wdec': jax.random.normal(ks[5], (H, D), f) * s, 'Wmix': jax.random.normal(ks[6], (H, D), f) * s, 'mix_bias': jnp.zeros((H,), f), 'wq_conv': jax.random.normal(ks[7], (D, K), f) * 0.3, 'wk_conv': jax.random.normal(ks[8], (D, K), f) * 0.3, 'wv_conv': jax.random.normal(ks[9], (D, K), f) * 0.3, 'onorm_w': jnp.ones((D // H,), f), 'Wo': jax.random.normal(ks[10], (D, D), f) * s}
    _L0_attn_in = _L0_attn_setup()

    def _L0_ffn_setup():
        import jax, jax.numpy as jnp
        import numpy as np
        key = jax.random.key(seed)
        ks = jax.random.split(key, 5)
        B, T, D, E = (4, 256, 128, 8)
        inputs = jax.random.normal(ks[0], (B, T, D), dtype=jnp.float32)
        Wr = jax.random.normal(ks[1], (D, E), dtype=jnp.float32) * 0.02
        br = jnp.zeros((E,), dtype=jnp.float32)
        W1 = jax.random.normal(ks[2], (E, D, D), dtype=jnp.float32) * 0.02
        b1 = jnp.zeros((E, D), dtype=jnp.float32)
        W2 = jax.random.normal(ks[3], (E, D, D), dtype=jnp.float32) * 0.02
        b2 = jnp.zeros((E, D), dtype=jnp.float32)
        return {'inputs': inputs, 'Wr': Wr, 'br': br, 'W1': W1, 'b1': b1, 'W2': W2, 'b2': b2}
    _L0_ffn_in = _L0_ffn_setup()
    _d = {'L0_attn_hidden_states': _L0_attn_in['hidden_states'], 'L0_attn_Wq': _L0_attn_in['Wq'], 'L0_attn_Wk': _L0_attn_in['Wk'], 'L0_attn_Wv': _L0_attn_in['Wv'], 'L0_attn_Wb': _L0_attn_in['Wb'], 'L0_attn_Wdec': _L0_attn_in['Wdec'], 'L0_attn_Wmix': _L0_attn_in['Wmix'], 'L0_attn_mix_bias': _L0_attn_in['mix_bias'], 'L0_attn_wq_conv': _L0_attn_in['wq_conv'], 'L0_attn_wk_conv': _L0_attn_in['wk_conv'], 'L0_attn_wv_conv': _L0_attn_in['wv_conv'], 'L0_attn_onorm_w': _L0_attn_in['onorm_w'], 'L0_attn_Wo': _L0_attn_in['Wo'], 'L0_ffn_Wr': _L0_ffn_in['Wr'], 'L0_ffn_br': _L0_ffn_in['br'], 'L0_ffn_W1': _L0_ffn_in['W1'], 'L0_ffn_b1': _L0_ffn_in['b1'], 'L0_ffn_W2': _L0_ffn_in['W2'], 'L0_ffn_b2': _L0_ffn_in['b2']}
    _x0 = _d['L0_attn_hidden_states']
    _d['L0_attn_hidden_states'] = jax.random.normal(jax.random.fold_in(jax.random.key(seed), 1), (2, 2048, 128), dtype=_x0.dtype)
    del _x0
    return _d

def reference(L0_attn_hidden_states, L0_attn_Wq, L0_attn_Wk, L0_attn_Wv, L0_attn_Wb, L0_attn_Wdec, L0_attn_Wmix, L0_attn_mix_bias, L0_attn_wq_conv, L0_attn_wk_conv, L0_attn_wv_conv, L0_attn_onorm_w, L0_attn_Wo, L0_ffn_Wr, L0_ffn_br, L0_ffn_W1, L0_ffn_b1, L0_ffn_W2, L0_ffn_b2):

    def _L0_attn_ref(hidden_states, Wq, Wk, Wv, Wb, Wdec, Wmix, mix_bias, wq_conv, wk_conv, wv_conv, onorm_w, Wo):
        import jax, jax.numpy as jnp
        import numpy as np
        CHUNK = 32
        EPS_L2 = 1e-06
        EPS_RMS = 1e-05
        NUM_HEADS = 4

        def _causal_dwconv_silu(x, w):
            k = w.shape[1]
            l = x.shape[1]
            xp = jnp.pad(x, ((0, 0), (k - 1, 0), (0, 0)))
            out = sum((w[:, j] * xp[:, j:j + l, :] for j in range(k)))
            return jax.nn.silu(out)

        def _l2norm(x):
            return x * jax.lax.rsqrt(jnp.sum(x * x, -1, keepdims=True) + EPS_L2)

        def _delta_rule_chunkwise(q, k, v, beta, c=CHUNK):
            b, h, l, dk = q.shape
            dv = v.shape[-1]
            n = l // c
            q = _l2norm(q)
            k = _l2norm(k)
            v = v * beta[..., None]
            kb = k * beta[..., None]
            qc = q.reshape(b, h, n, c, dk)
            kc = k.reshape(b, h, n, c, dk)
            vc = v.reshape(b, h, n, c, dv)
            kbc = kb.reshape(b, h, n, c, dk)
            strict_lower = jnp.tril(jnp.ones((c, c), bool), -1)
            attn = -jnp.einsum('bhnik,bhnjk->bhnij', kbc, kc)
            attn = jnp.where(strict_lower, attn, 0.0)
            for i in range(1, c):
                upd = jnp.einsum('bhnj,bhnjm->bhnm', attn[..., i, :], attn[..., :, :i])
                attn = attn.at[..., i, :i].add(upd)
            attn = attn + jnp.eye(c, dtype=attn.dtype)
            u = attn @ vc
            w = attn @ kbc
            incl_lower = jnp.tril(jnp.ones((c, c), bool))

            def step(S, inp):
                q_i, k_i, u_i, w_i = inp
                a = jnp.where(incl_lower, jnp.einsum('bhik,bhjk->bhij', q_i, k_i), 0.0)
                u_new = u_i - w_i @ S
                o_i = q_i @ S + a @ u_new
                S = S + jnp.einsum('bhck,bhcv->bhkv', k_i, u_new)
                return (S, o_i)
            S0 = jnp.zeros((b, h, dk, dv), q.dtype)
            xs = tuple((jnp.moveaxis(x, 2, 0) for x in (qc, kc, u, w)))
            S, o = jax.lax.scan(step, S0, xs)
            o = jnp.moveaxis(o, 0, 2).reshape(b, h, l, dv)
            return (o, S)

        def _ema(v, gamma):
            vt = jnp.moveaxis(v, 2, 0)
            gt = jnp.moveaxis(gamma, 2, 0)[..., None]

            def step(s, xg):
                x, g = xg
                s = g * s + (1.0 - g) * x
                return (s, s)
            s0 = jnp.zeros(v.shape[:2] + v.shape[-1:], v.dtype)
            _, out = jax.lax.scan(step, s0, (vt, gt))
            return jnp.moveaxis(out, 0, 2)

        def _forward(hs, Wq, Wk, Wv, Wb, Wdec, Wmix, mix_bias, wq_conv, wk_conv, wv_conv, onorm_w, Wo):
            b, l, d = hs.shape
            h = NUM_HEADS
            q = _causal_dwconv_silu(hs @ Wq.T, wq_conv)
            k = _causal_dwconv_silu(hs @ Wk.T, wk_conv)
            v = _causal_dwconv_silu(hs @ Wv.T, wv_conv)
            dk = q.shape[-1] // h
            dv = v.shape[-1] // h
            q = q.reshape(b, l, h, dk)
            k = k.reshape(b, l, h, dk)
            v = v.reshape(b, l, h, dv)
            beta = jax.nn.sigmoid(hs @ Wb.T)
            qd = jnp.transpose(q, (0, 2, 1, 3))
            kd = jnp.transpose(k, (0, 2, 1, 3))
            vd = jnp.transpose(v, (0, 2, 1, 3))
            bd = jnp.transpose(beta, (0, 2, 1))
            o_d, _S = _delta_rule_chunkwise(qd, kd, vd, bd)
            o_d = jnp.transpose(o_d, (0, 2, 1, 3))
            gamma = jnp.transpose(jax.nn.sigmoid(hs @ Wdec.T), (0, 2, 1))
            ema_out = jnp.transpose(_ema(vd, gamma), (0, 2, 1, 3))
            mix = jax.nn.sigmoid(hs @ Wmix.T + mix_bias)[..., None]
            o = (1.0 - mix) * o_d + mix * ema_out
            o = o * jax.lax.rsqrt(jnp.mean(o * o, -1, keepdims=True) + EPS_RMS) * onorm_w
            return o.reshape(b, l, h * dv) @ Wo.T
        return _forward(hidden_states, Wq, Wk, Wv, Wb, Wdec, Wmix, mix_bias, wq_conv, wk_conv, wv_conv, onorm_w, Wo)

    def _L0_ffn_ref(inputs, Wr, br, W1, b1, W2, b2):
        import jax, jax.numpy as jnp
        import numpy as np
        B, T, D = inputs.shape
        E = Wr.shape[1]
        x = inputs.reshape(B * T, D)
        N = x.shape[0]
        C = N // E
        logits = x @ Wr + br
        probs = jax.nn.softmax(logits, axis=-1)
        gate = jnp.max(probs, axis=-1, keepdims=True)
        idx = jnp.argmax(probs, axis=-1)
        mask = jax.nn.one_hot(idx, E, dtype=jnp.float32)
        pos = (jnp.cumsum(mask, axis=0) * mask).astype(jnp.int32)
        mask = mask * (pos < C).astype(jnp.float32)
        mask_flat = jnp.sum(mask, axis=-1, keepdims=True)
        gate = gate * mask_flat
        combine = (gate * mask_flat * jax.nn.one_hot(idx, E, dtype=jnp.float32))[..., None] * jax.nn.one_hot(pos, C, dtype=jnp.float32)
        dispatch = combine
        expert_in = jnp.einsum('nd,nec->ecd', x, dispatch)
        h = jax.nn.relu(jnp.einsum('ecd,edf->ecf', expert_in, W1) + b1[:, None, :])
        eo = jnp.einsum('ecf,efd->ecd', h, W2) + b2[:, None, :]
        out = jnp.einsum('ecd,nec->nd', eo, combine)
        return out.reshape(B, T, D)
    x = L0_attn_hidden_states
    x = x + 0.5 * _L0_ffn_ref(_layernorm(x, axis=-1), L0_ffn_Wr, L0_ffn_br, L0_ffn_W1, L0_ffn_b1, L0_ffn_W2, L0_ffn_b2)
    x = x + _L0_attn_ref(_layernorm(x, axis=-1), L0_attn_Wq, L0_attn_Wk, L0_attn_Wv, L0_attn_Wb, L0_attn_Wdec, L0_attn_Wmix, L0_attn_mix_bias, L0_attn_wq_conv, L0_attn_wk_conv, L0_attn_wv_conv, L0_attn_onorm_w, L0_attn_Wo)
    x = x + 0.5 * _L0_ffn_ref(_layernorm(x, axis=-1), L0_ffn_Wr, L0_ffn_br, L0_ffn_W1, L0_ffn_b1, L0_ffn_W2, L0_ffn_b2)
    return x

_drawn_inputs = setup_inputs


def setup_inputs(seed=0):
    import zlib

    import numpy as np

    out = dict(_drawn_inputs(seed))
    spreads = {'L0_attn_mix_bias': (0.0, 0.8),
     'L0_attn_onorm_w': (1.0, 0.2),
     'L0_ffn_br': (0.0, 0.575),
     'L0_ffn_b1': (0.0, 0.8),
     'L0_ffn_b2': (0.0, 0.614)}
    factors = {'L0_attn_Wb': 2.994,
     'L0_attn_Wdec': 2.833,
     'L0_ffn_Wr': 4.639,
     'L0_ffn_W1': 8.0,
     'L0_ffn_W2': 8.0}
    for name, (base, spread) in spreads.items():
        noise = np.random.default_rng([zlib.crc32(name.encode()), seed]).standard_normal(out[name].shape)
        drawn = base * np.exp(spread * noise) if base else spread * noise
        out[name] = jnp.asarray(drawn.astype(out[name].dtype))
    for name, factor in factors.items():
        out[name] = (out[name] * factor).astype(out[name].dtype)
    return out
```

```python
import concourse.bass as bass
from concourse import mybir
from contextlib import ExitStack

F32 = mybir.dt.float32
BF16 = mybir.dt.bfloat16
U32 = mybir.dt.uint32
ALU = mybir.AluOpType
ACT = mybir.ActivationFunctionType
AX_X = mybir.AxisListType.X
ds = bass.ds

P = 128
CH = 32
EPS_LN = 1e-5
EPS_L2 = 1e-6
EPS_RMS = 1e-5


class Steps:

    def __init__(self, eng, sem):
        self.eng, self.sem = eng, sem
        self.base, self.local, self.reg, self.per = 0, 0, None, 0

    def did(self, instruction):
        instruction.then_inc(self.sem, 1)
        self.local += 1
        return instruction

    def value(self, back=0):
        v = self.base + self.local - back
        return v if self.reg is None else (self.reg - self.first) * (self.per // self.step) + v

    def wait(self, back=0):
        self.eng.wait_ge(self.sem, self.value(back))

    def enter(self, reg, first, per, step=1):
        assert per % step == 0
        self.base += self.local
        self.reg, self.first, self.per, self.step, self.local = reg, first, per, step, 0

    def leave(self, times):
        assert self.local == self.per, (self.local, self.per)
        self.base += self.per * times
        self.reg, self.local = None, 0


def macaron_kernel(nc, t, out, stop=99, dump=None):
    x_d = t["L0_attn_hidden_states"]
    B, L, D = x_d.shape
    H = t["L0_attn_Wb"].shape[0]
    KT = t["L0_attn_wq_conv"].shape[1]
    E = t["L0_ffn_Wr"].shape[1]
    N = B * L
    CAP = N // E
    NT = N // P
    TG = 4
    NG = NT // TG
    SG = L // 512
    NO = L // P
    M = 2 * 512 // CH
    R = H * CH
    assert (B, D, H * CH, CAP, R, M) == (2, P, P, 512, P, 32)

    x_v = x_d.rearrange("b (t p) d -> p (b t) d", p=P)
    out_v = out.rearrange("b (t p) d -> p (b t) d", p=P)
    slots_d = nc.dram_tensor("expert_rows", [2 * N, D], F32).ap()
    eout_d = nc.dram_tensor("expert_out", [N, D], F32).ap()
    slots_v = slots_d[0:N, :].rearrange("(e p s) d -> e p (s d)", p=P, s=CAP // P)
    eout_v = eout_d.rearrange("(e p s) d -> e p (s d)", p=P, s=CAP // P)

    ctx = ExitStack()
    with ctx:
        def sb(name, shape, dt=F32):
            return ctx.enter_context(nc.sbuf_tensor(name, shape, dt))

        sems = {}

        def sem(name):
            if name not in sems:
                sems[name] = ctx.enter_context(nc.semaphore(name))
            return sems[name]

        ps = [ctx.enter_context(nc.psum_tensor(f"bank{i}", [P, 512], F32)) for i in range(8)]

        X = sb("X", [P, NT, D])
        XG = sb("XG", [P, NT, D])
        XNT = sb("XNT", [P, B, L + KT - 1])
        VKA = sb("VKA", [P, NO * 8, 96])
        QN = sb("QN", [P, NO * 8, CH])
        EM = sb("EM", [P, B, L])
        MX = sb("MX", [P, B, L])
        W = [sb(f"W{i}", [P, 1024]) for i in range(11)]
        KQ = sb("KQ", [P, M, 64])
        TT = XG[:, :, :].rearrange("p t d -> p (t d)")

        ident = sb("ident", [P, P])
        bdm = sb("bdm", [P, H, CH])
        negbd = sb("negbd", [P, H, CH])
        triu = sb("triu", [P, CH])
        cw = sb("cw", [P, 3 * KT, P])
        gw = sb("gw", [P, 3, P])
        wo = sb("wo", [P, P])
        mbias = sb("mbias", [P, 1])
        onw = sb("onw", [P, 1])
        ceps = sb("ceps", [P, 2])
        mhalf = sb("mhalf", [P, 2 * M])
        mean = sb("mean", [P, NT])
        var = sb("var", [P, NT])
        rstd = sb("rstd", [P, NT])
        Sst = sb("Sst", [P, B * CH])
        SBs = sb("SBs", [P, B * CH])
        rn = sb("rn", [P, 2, M])
        nb = sb("nb", [P, M])

        arena = VKA[:, :, :].rearrange("p m c -> p (m c)")
        used = [0]

        def part(n):
            used[0] += n
            assert used[0] <= NO * 8 * 96
            return arena[:, used[0] - n:used[0]]

        XE = part(2 * 512).rearrange("p (r s d) -> p r s d", r=2, s=4)
        EO = part(2 * 512).rearrange("p (r s d) -> p r s d", r=2, s=4)
        HT = part(2 * 512).rearrange("p (r n) -> p r n", r=2)
        XET = part(2 * 512).rearrange("p (r n) -> p r n", r=2)
        W1 = part(2 * 128).rearrange("p (r n) -> p r n", r=2)
        W2 = part(E * D).rearrange("p (e n) -> p e n", e=E)
        B2 = part(E * D).rearrange("p (e n) -> p e n", e=E)
        B1 = part(E)
        wr = part(E)
        brb = part(E)
        st = part(NT * 6).rearrange("p (t x) -> p t x", x=6)
        XN4 = part(TG * D).rearrange("p (t d) -> p t d", t=TG)
        YT4 = part(TG * D).rearrange("p (t d) -> p t d", t=TG)
        te = lambda: part(NT * E).rearrange("p (t e) -> p t e", e=E)
        lg, eq, ex, cum = te(), te(), te(), te()
        tot, incl, rmask, eoff = part(NT * E), part(NT * E), part(NT * E), part(NT * E)
        mx, sm, gate, keep, hgate, slot, trash, tmp1, mrev = [part(NT) for _ in range(9)]
        rev = part(E)
        sidx = part(NT).bitcast(U32)
        gidx = part(NT).bitcast(U32)
        i1 = part(NT * E).bitcast(mybir.dt.int32)
        oh = part(NT * E // 2).bitcast(BF16).rearrange("p (t e) -> p t e", e=E)
        tri = part(P // 2).bitcast(BF16)
        onesb = part(P // 2).bitcast(BF16)

        def eview(a):
            return a.rearrange("p (e t) -> p t e", e=E)

        def bt(i):
            return W[i][:, :].rearrange("p (b l) -> p b l", b=B)
        qT, kT, vT, ga, gb, be = [bt(i) for i in range(6)]
        qC, kC, vC, bC = [W[i][:, :].rearrange("p (m d) -> p m d", d=CH) for i in (6, 7, 8, 9)]
        sqq = KQ[:, 0:M // 2, :].rearrange("p m d -> p (m d)").rearrange("p (m d) -> p m d", d=CH)
        sqk = KQ[:, M // 2:M, :].rearrange("p m d -> p (m d)").rearrange("p (m d) -> p m d", d=CH)
        AG = qC
        RA = W[7][:, :].rearrange("p (j i) -> p j i", j=CH)
        RT = W[8][:, :].rearrange("p (i c) -> p i c", c=CH)
        TC = qC
        KB = W[10][:, :].rearrange("p (r c h d) -> p r c h d", r=2, c=4, h=H)
        prod = W[6]

        BDT = W[0][:, :].rearrange("p (c h d) -> p c h d", c=8, h=H)
        BDU = W[1][:, :].rearrange("p (c h d) -> p c h d", c=8, h=H)
        BDW = W[2][:, :].rearrange("p (c h d) -> p c h d", c=8, h=H)
        BDP = W[3][:, :].rearrange("p (c h d) -> p c h d", c=8, h=H)
        Bc = W[4][:, 0:256].rearrange("p (c d) -> p c d", d=CH)
        BDS = [W[5][:, :].rearrange("p (c h d) -> p c h d", c=8, h=H),
               W[6][:, :].rearrange("p (c h d) -> p c h d", c=8, h=H)]
        f256 = lambda w, k: W[w][:, 256 * k:256 * k + 256].rearrange("p (b x) -> p b x", b=B)
        o1 = [f256(7, 0), f256(7, 1)]
        o2 = [f256(7, 2), f256(7, 3)]
        o3 = [f256(8, 0), f256(8, 1)]
        osq = [f256(8, 2), f256(8, 3)]
        ors = [f256(9, 0), f256(9, 1)]
        on = [f256(9, 2), f256(9, 3)]

        def ffn_sems(k):
            return {n: sem(f"{n}{k}") for n in (
                "mean_steps", "var_ready", "std_ready", "xn_ready", "xn_turned", "xnT_taken",
                "logits_done", "z_ready", "exp_ready", "onehot_ready", "ranks_done", "rows_ready",
                "scattered", "w1_used", "rows_used", "rows_turned", "rowsT_ready", "hidden_done",
                "hidden_ready", "eout_done", "eout_ready", "added")} | {
                n: [sem(f"{n}{k}_{r}") for r in range(2)] for n in ("w1_in", "rows_in", "stored")}

        x_in = sem("x_in")
        w_in = sem("w_in")
        fw_in = sem("fw_in")
        zero_ready = sem("zero_ready")
        zeroed = sem("zeroed")
        consts = sem("consts")
        w_scaled = sem("w_scaled")
        w_turned = sem("w_turned")
        w_taken = sem("w_taken")
        NWT = 3 * KT + 4

        block = ctx.enter_context(nc.Block())

        wsrc = [(t["L0_attn_Wq"], t["L0_attn_wq_conv"]), (t["L0_attn_Wk"], t["L0_attn_wk_conv"]),
                (t["L0_attn_Wv"], t["L0_attn_wv_conv"])]
        wraw = W[0][:, 0:3 * P].rearrange("p (n d) -> p n d", n=3)
        graw = W[0][:, 3 * P:6 * P].rearrange("p (n d) -> p n d", n=3)
        woraw = W[0][:, 6 * P:7 * P]
        craw = W[0][:, 7 * P:7 * P + 3 * KT].rearrange("p (n j) -> p n j", n=3)
        wsc = [W[1 + n // 8][:, P * (n % 8):P * (n % 8) + P] for n in range(3 * KT)]

        locals_ = locals()
        @block.sync
        def _(sp):
            sp.dma_start(X[:, 0:NT // 2, :], x_v[:, 0:NT // 2, :]).then_inc(x_in, 16)
            sp.dma_start(X[:, NT // 2:NT, :], x_v[:, NT // 2:NT, :]).then_inc(x_in, 16)
            with nc.allow_non_contiguous_dma(reason="small"):
                sp.dma_start(wr, t["L0_ffn_Wr"]).then_inc(fw_in, 16)
                sp.dma_start(brb, t["L0_ffn_br"].rearrange("(a e) -> a e", a=1).broadcast_to([P, E])).then_inc(fw_in, 16)
                sp.dma_start(B1, t["L0_ffn_b1"].rearrange("e f -> f e")).then_inc(fw_in, 16)
                sp.dma_start(B2, t["L0_ffn_b2"].rearrange("(a e) d -> a e d", a=1).broadcast_to([P, E, D])).then_inc(fw_in, 16)
                sp.dma_start(W2, t["L0_ffn_W2"].rearrange("e f d -> f e d")).then_inc(fw_in, 16)
                for n, (w, c) in enumerate(wsrc):
                    sp.dma_start(wraw[:, n, :], w).then_inc(w_in, 16)
                    sp.dma_start(craw[:, n, :], c).then_inc(w_in, 16)
                for n, w in enumerate(("L0_attn_Wdec", "L0_attn_Wb", "L0_attn_Wmix")):
                    for h in range(H):
                        sp.dma_start(graw[CH * h:CH * h + CH, n, :], t[w][h:h + 1, :].broadcast_to([CH, D])).then_inc(w_in, 16)
                sp.dma_start(woraw, t["L0_attn_Wo"]).then_inc(w_in, 16)
                for h in range(H):
                    sp.dma_start(mbias[CH * h:CH * h + CH, :], t["L0_attn_mix_bias"].rearrange("(h a) -> h a", a=1)[h:h + 1, :].broadcast_to([CH, 1])).then_inc(w_in, 16)
                    sp.dma_start(onw[CH * h:CH * h + CH, :], t["L0_attn_onorm_w"].rearrange("(d a) -> d a", a=1)).then_inc(w_in, 16)
            sp.wait_ge(zero_ready, 1)
            for e in range(E):
                sp.dma_start(slots_v[e], XG[:, 4 * e:4 * e + 4, :].rearrange("p s d -> p (s d)")).then_inc(zeroed, 16)

            def ffn_io(k):
                s = ffn_sems(k)

                def load(j, r):
                    e = j * 2 + r
                    if not isinstance(j, int):
                        sp.wait_ge(s["w1_used"], e - 1)
                        sp.wait_ge(s["rows_used"], e - 1)
                    sp.dma_start(W1[:, r, :], t["L0_ffn_W1"][ds(e, 1)].rearrange("e d f -> (e d) f")).then_inc(s["w1_in"][r], 16)
                    sp.dma_start(XE[:, r].rearrange("p s d -> p (s d)"),
                                 slots_v[ds(e, 1)].rearrange("e p x -> (e p) x")).then_inc(s["rows_in"][r], 16)

                def store(j, r):
                    e = j * 2 + r
                    sp.wait_ge(s["eout_ready"], e + 1)
                    sp.dma_start(eout_v[ds(e, 1)].rearrange("e p x -> (e p) x"),
                                 EO[:, r].rearrange("p s d -> p (s d)")).then_inc(s["stored"][r], 16)
                if k:
                    sp.wait_ge(sem("attn_done"), 1)
                    for dst, name in ((wr, "L0_ffn_Wr"),):
                        sp.dma_start(dst, t[name]).then_inc(fw_in, 16)
                    with nc.allow_non_contiguous_dma(reason="small"):
                        sp.dma_start(brb, t["L0_ffn_br"].rearrange("(a e) -> a e", a=1).broadcast_to([P, E])).then_inc(fw_in, 16)
                        sp.dma_start(B1, t["L0_ffn_b1"].rearrange("e f -> f e")).then_inc(fw_in, 16)
                        sp.dma_start(B2, t["L0_ffn_b2"].rearrange("(a e) d -> a e d", a=1).broadcast_to([P, E, D])).then_inc(fw_in, 16)
                        sp.dma_start(W2, t["L0_ffn_W2"].rearrange("e f d -> f e d")).then_inc(fw_in, 16)
                sp.wait_ge(s["scattered"], 16 * NT)
                load(0, 0)
                load(0, 1)
                with sp.Fori(0, E // 2 - 1) as j:
                    for r in range(2):
                        store(j, r)
                        load(j + 1, r)
                store(E // 2 - 1, 0)
                store(E // 2 - 1, 1)

            if stop >= 1:
                ffn_io(0)
            if stop >= 5:
                ffn_io(1)
            if dump is not None:
                sp.wait_ge(sem("fin"), 1)
                sp.dma_start(out_v, dump(locals_)).then_inc(sem("out_in"), 16)
                sp.wait_ge(sem("out_in"), 16)
            else:
                with sp.Fori(0, NG) as g:
                    sp.wait_ge(sem("added1"), g * TG + TG)
                    sp.dma_start(out_v[:, ds(g * TG, TG), :], X[:, ds(g * TG, TG), :]).then_inc(sem("out_in"), 16)
                sp.wait_ge(sem("out_in"), 16 * NG)

        @block.gpsimd
        def _(pool):
            g = nc.gpsimd
            sp_ = Steps(pool, sem("pool_steps"))

            def one(instruction):
                sp_.did(instruction)
                sp_.wait()

            def make_consts():
                one(g.memset(ident[:, :], 0.0))
                one(g.memset(bdm[:, :, :], 0.0))
                one(g.memset(triu[:, :], 1.0))
                one(g.memset(ceps[:, 0:1], EPS_LN))
                one(g.memset(ceps[:, 1:2], EPS_RMS))
                one(g.memset(mhalf[:, :], -0.5))
                one(g.memset(XNT[:, :, 0:KT - 1], 0.0))
                one(g.affine_select(out=ident[:, :], in_=ident[:, :], compare_op=ALU.not_equal, fill=1.0,
                                base=0, pattern=[[-1, P]], channel_multiplier=1))
                for h in range(H):
                    q = slice(CH * h, CH * h + CH)
                    one(g.memset(bdm[q, h, :], 1.0))
                    one(g.affine_select(out=triu[q, :], in_=triu[q, :], compare_op=ALU.is_ge, fill=0.0,
                                    base=0, pattern=[[1, CH]], channel_multiplier=-1))
                one(g.tensor_scalar(negbd[:, :, :], bdm[:, :, :], -1.0, None, ALU.mult))

            def ffn_consts(k):
                one(g.memset(onesb, 1.0))
                one(g.memset(tri, 1.0))
                one(g.memset(rmask, 1.0))
                one(g.affine_select(out=tri, in_=tri, compare_op=ALU.is_ge, fill=0.0, base=0,
                                pattern=[[1, P]], channel_multiplier=-1))
                one(g.memset(rmask.rearrange("p (e t) -> p e t", e=E)[:, :, 0:1], 0.0))
                one(g.iota(i1[:, 0:E], pattern=[[-1, E]], base=E, channel_multiplier=0))
                one(g.tensor_copy(rev, i1[:, 0:E]))
                one(g.iota(i1[:, 0:NT], pattern=[[P, NT]], base=N, channel_multiplier=1))
                one(g.tensor_copy(trash, i1[:, 0:NT]))
                one(g.iota(i1, pattern=[[CAP, E], [0, NT]], base=0, channel_multiplier=0))
                g.tensor_copy(eoff, i1).then_inc(consts, 1)

            make_consts()
            ffn_consts(0)

            def ffn_moves(k):
                s = ffn_sems(k)
                if k == 0:
                    pool.wait_ge(zeroed, 16 * E)
                for n in range(NT):
                    pool.wait_ge(s["rows_ready"], n + 1)
                    g.indirect_dma_start(slots_d, bass.IndirectOffsetOnAxis(ap=sidx[:, n:n + 1], axis=0),
                                         XG[:, n, :], None).then_inc(s["scattered"], 16)
                for r in range(2):
                    pool.wait_ge(s["stored"][r], 16 * (E // 2))
                for n in range(NT):
                    g.indirect_dma_start(XG[:, n, :], None, eout_d,
                                         bass.IndirectOffsetOnAxis(ap=gidx[:, n:n + 1], axis=0)).then_inc(
                                             sem(f"gathered{k}_{n // TG}"), 16)

            if stop >= 1:
                ffn_moves(0)

            def span(s, first):
                pool.wait_ge(sem("qk_chunked"), 2 * s + 1)
                g.tensor_tensor(sqq, qC, qC, ALU.mult).then_inc(sem("sq_ready"), 1)
                pool.wait_ge(sem("qk_chunked"), 2 * s + 2)
                g.tensor_tensor(sqk, kC, kC, ALU.mult).then_inc(sem("sq_ready"), 1)
                pool.wait_ge(sem("ss_ready"), s + 1)
                g.tensor_tensor(rn[:, :, :], rn[:, :, :], mhalf[:, :].rearrange("p (a m) -> p a m", a=2),
                                ALU.pow).then_inc(sem("rn_ready"), 1)
                pool.wait_ge(sem("silu_ready"), 6 * s + 6)
                pool.wait_ge(sem("gates_ready"), 8 * s + 4)
                g.tensor_tensor(gb, gb, vT, ALU.mult).then_inc(sem("gv_ready"), 1)
                pool.wait_ge(sem("kq_ready"), s + 1)
                for n in range(M // 4):
                    if not first or n >= 2:
                        pool.wait_ge(sem("gram_half"), 8 * s + n - 1)
                    g.tensor_tensor(KB[:, n % 2], KQ[:, 4 * n:4 * n + 4, 0:CH].unsqueeze(2).to_broadcast([P, 4, H, CH]),
                                    bdm[:, :, :].unsqueeze(1).to_broadcast([P, 4, H, CH]), ALU.mult).then_inc(sem("kb_ready"), 1)

            if stop >= 2:
                span(0, True)
                with pool.Fori(1, SG) as i:
                    span(i, False)

            if stop >= 3:
                pool.wait_ge(sem("tt_ready"), SG)
                pool.wait_ge(sem("uw_cleared"), 1)

                def bdt(o, first):
                    if not first:
                        pool.wait_ge(sem("wu_done"), 2 * o)
                    g.tensor_tensor(BDT, TT[:, ds(o * 256, 256)].rearrange("p (c d) -> p c d", d=CH).unsqueeze(2).to_broadcast([P, 8, H, CH]),
                                    bdm[:, :, :].unsqueeze(1).to_broadcast([P, 8, H, CH]), ALU.mult).then_inc(sem("bdt_ready"), 1)
                bdt(0, True)
                with pool.Fori(1, NO) as i:
                    bdt(i, False)

            if stop >= 4:
                def states(o, r, first):
                    if not first:
                        pool.wait_ge(sem("od_done"), o - 1)
                    g.tensor_tensor(BDS[r], VKA[:, ds(o * 8, 8), CH:2 * CH].unsqueeze(2).to_broadcast([P, 8, H, CH]),
                                    bdm[:, :, :].unsqueeze(1).to_broadcast([P, 8, H, CH]), ALU.mult).then_inc(sem("bds_ready"), 1)

                def mixing(o, r):
                    pool.wait_ge(sem("od_ready"), o + 1)
                    if not (isinstance(o, int) and o < 2):
                        pool.wait_ge(sem("o_ready"), o - 1)
                    g.tensor_tensor(o2[r], EM[:, :, ds(o * P, P)], o1[r], ALU.subtract).then_inc(sem("pool_mix"), 1)
                    pool.wait_ge(sem("pool_mix"), o + 1)
                    g.tensor_tensor(o2[r], o2[r], MX[:, :, ds(o * P, P)], ALU.mult).then_inc(sem("mix_ready"), 1)
                pool.wait_ge(sem("state_done"), NO * 4 + 1)
                states(0, 0, True)
                states(1, 1, True)
                for r in range(2):
                    mixing(r, r)
                    states(r + 2, r, False)
                with pool.Fori((2) // 2, (NO - 2) // 2) as j:
                    i = j * 2
                    for r in range(2):
                        mixing(i + r, r)
                        states(i + r + 2, r, False)
                mixing(NO - 2, 0)
                mixing(NO - 1, 1)
            if stop >= 5:
                pool.wait_ge(sem("attn_done"), 1)
                ffn_consts(1)
                ffn_moves(1)

        @block.tensor
        def _(pe):
            mm = nc.tensor.matmul
            tr = nc.tensor.transpose

            def turn_weights():
                pe.wait_ge(consts, 1)
                for n in range(NWT):
                    pe.wait_ge(w_scaled, min(n + 1, 3 * KT))
                    src = wsc[n] if n < 3 * KT else (graw[:, n - 3 * KT, :] if n < NWT - 1 else woraw)
                    if n >= 4:
                        pe.wait_ge(w_taken, n - 3)
                    tr(ps[n % 4][:, 0:P], src, ident[:, :]).then_inc(w_turned, 1)

            def turn_group(s, first, g):
                pe.wait_ge(s["xn_ready"], g * TG + TG)
                if not first:
                    pe.wait_ge(s["xnT_taken"], g)
                for k in range(TG):
                    last = tr(ps[4][:, P * k:P * k + P], XN4[:, k, :], ident[:, :])
                last.then_inc(s["xn_turned"], 1)

            def ffn(k):
                s = ffn_sems(k)
                pe.wait_ge(fw_in, 16 * 5 * (k + 1))

                def front(g, first):
                    turn_group(s, first, g)
                    pe.wait_ge(s["xnT_taken"], g + 1)
                    for j in range(TG):
                        last = mm(ps[5][:, ds(g * (TG * E) + j * E, E)], YT4[:, j, :], wr, start=True, stop=True)
                    last.then_inc(s["logits_done"], 1)
                front(0, True)
                with pe.Fori(1, NG) as g:
                    front(g, False)
                pe.wait_ge(s["onehot_ready"], 1)
                mm(ps[6][:, 0:NT * E], tri, oh.rearrange("p t e -> p (t e)"), start=True, stop=True)
                mm(ps[7][:, 0:NT * E], onesb, oh.rearrange("p t e -> p (t e)"), start=True, stop=True).then_inc(s["ranks_done"], 1)

                def expert(j, r, first):
                    e = j * 2 + r
                    pe.wait_ge(s["rows_in"][r], j * 16 + 16)
                    for c in range(4):
                        last = tr(ps[r][:, P * c:P * c + P], XE[:, r, c, :], ident[:, :])
                    last.then_inc(s["rows_used"], 1)
                    pe.wait_ge(s["w1_in"][r], j * 16 + 16)
                    pe.wait_ge(s["rowsT_ready"], e + 1)
                    mm(ps[2 + r][:, :], W1[:, r, :], XET[:, r, :], start=True, stop=True).then_inc(s["w1_used"], 1)
                    pe.wait_ge(s["hidden_ready"], e + 1)
                    if not first:
                        pe.wait_ge(s["eout_ready"], e - 1)
                    for c in range(4):
                        last = mm(ps[4 + r][:, P * c:P * c + P], HT[:, r, P * c:P * c + P], W2[:, ds(e, 1), :].rearrange("p e d -> p (e d)"),
                                  start=True, stop=True)
                    last.then_inc(s["eout_done"], 1)
                expert(0, 0, True)
                expert(0, 1, True)
                with pe.Fori(1, E // 2) as j:
                    for r in range(2):
                        expert(j, r, False)

            turn_weights()
            if stop >= 1:
                ffn(0)

            NP = 12

            def project(s, first):
                for n in range(NP):
                    kind, b = n // 2, n % 2
                    if not (first and n < 4):
                        pe.wait_ge(sem("proj_free"), s * NP + n - 3)
                    if kind < 3:
                        for j in range(KT):
                            last = mm(ps[n % 4][:, :], cw[:, kind * KT + j, :], XNT[:, b, ds(s * 512 + j, 512)],
                                      start=j == 0, stop=j == KT - 1)
                    else:
                        last = mm(ps[n % 4][:, :], gw[:, kind - 3, :], XNT[:, b, ds(s * 512 + KT - 1, 512)],
                                  start=True, stop=True)
                    last.then_inc(sem("proj_done"), 1)

            def gram(s, first):
                for n in range(M // 4):
                    pe.wait_ge(sem("kb_ready"), 8 * s + n + 1)
                    if n % 2 == 0 and not (first and n < 4):
                        pe.wait_ge(sem("gram_taken"), 4 * s + n // 2 - 1)
                    for c in range(4):
                        m = 4 * n + c
                        k = (n % 2) * 256 + c * 64
                        last = mm(ps[4 + (n // 2) % 2][:, k:k + 64], KB[:, n % 2, c].rearrange("p h d -> p (h d)"),
                                  KQ[:, m, :], start=True, stop=True)
                    last.then_inc(sem("gram_half"), 1)

            if stop >= 2:
                s = {n: sem(f"{n}_a") for n in ("xn_ready", "xnT_taken", "xn_turned")}
                turn_group(s, True, 0)
                with pe.Fori(1, NG) as g:
                    turn_group(s, False, g)
                pe.wait_ge(s["xnT_taken"], NG)
                project(0, True)
                project(1, False)
                gram(0, True)
                with pe.Fori(1, SG - 1) as i:
                    project(i + 1, False)
                    gram(i, False)
                gram(SG - 1, False)

            if stop >= 3:
                flat = lambda a: a.rearrange("p h d -> p (h d)")

                def wu(o, first):
                    pe.wait_ge(sem("bdt_ready"), o + 1)
                    for c in range(8):
                        if not first and c % 4 == 0:
                            pe.wait_ge(sem("uw_taken"), 2 * o + c // 4 - 1)
                        last = mm(ps[c // 4][:, 64 * (c % 4):64 * (c % 4) + 64], flat(BDT[:, c]),
                                  VKA[:, ds(o * 8 + c, 1), 0:64].rearrange("p m c -> p (m c)"), start=True, stop=True)
                        if c % 4 == 3:
                            last.then_inc(sem("wu_done"), 1)

                def mqbo(o, c, first):
                    if c % 4 == 0:
                        pe.wait_ge(sem("uw_taken"), 2 * o + c // 4 + 1)
                    if c == 0 and not first:
                        pe.wait_ge(sem("mq_taken"), o)
                    rhs = VKA[:, ds(o * 8 + c, 1), 32:96].rearrange("p m c -> p (m c)")
                    mm(ps[2][:, 64 * c:64 * c + 64], flat(BDW[:, c]), rhs, start=True, stop=True)
                    last = mm(ps[3][:, 64 * c:64 * c + 64], flat(BDU[:, c]), rhs, start=True, stop=True)
                    if c == 7:
                        last.then_inc(sem("mqbo_done"), 1)

                def chain(o, k):
                    if k == 0:
                        pe.wait_ge(sem("mq_taken"), o + 1)
                    pe.wait_ge(sem("state_done"), o * 4 + k + 1)
                    for b in range(B):
                        last = mm(ps[4 + k % 2][:, CH * b:CH * b + CH], flat(BDP[:, 4 * b + k]), Sst[:, CH * b:CH * b + CH],
                                  start=True, stop=True)
                    last.then_inc(sem("chain_done"), 1)

                wu(0, True)
                for c in range(8):
                    mqbo(0, c, True)
                with pe.Fori(1, NO) as o:
                    wu(o, False)
                    for k in range(4):
                        chain(o - 1, k)
                        mqbo(o, 2 * k, False)
                        mqbo(o, 2 * k + 1, False)
                for k in range(4):
                    chain(NO - 1, k)

            if stop >= 4:
                def outs(o, r, first):
                    pe.wait_ge(sem("bds_ready"), o + 1)
                    if not first:
                        pe.wait_ge(sem("od_ready"), o - 1)
                    for c in range(8):
                        last = mm(ps[r][:, CH * c:CH * c + CH], flat(BDS[r][:, c]), QN[:, ds(o * 8 + c, 1), :].rearrange("p m c -> p (m c)"),
                                  start=True, stop=True)
                    last.then_inc(sem("od_done"), 1)

                def norms(o, r, first):
                    pe.wait_ge(sem("osq_ready"), o + 1)
                    if not first:
                        pe.wait_ge(sem("ors_ready"), o - 1)
                    mm(ps[2 + r][:, 0:256], bdm[:, :, :].rearrange("p h d -> p (h d)"), osq[r].rearrange("p b x -> p (b x)"),
                       start=True, stop=True).then_inc(sem("oss_done"), 1)

                def proj_out(o, r, first):
                    pe.wait_ge(sem("on_ready"), o + 1)
                    if not first:
                        pe.wait_ge(sem("attn_added"), o - 1)
                    for b in range(B):
                        last = mm(ps[6 + r][:, P * b:P * b + P], on[r][:, b, :], wo[:, :], start=True, stop=True)
                    last.then_inc(sem("wo_done"), 1)
                outs(0, 0, True)
                outs(1, 1, True)
                norms(0, 0, True)
                outs(2, 0, False)
                norms(1, 1, True)
                proj_out(0, 0, True)
                outs(3, 1, False)
                norms(2, 0, False)
                proj_out(1, 1, True)
                with pe.Fori((4) // 2, (NO) // 2) as j:
                    o = j * 2
                    for r in range(2):
                        outs(o + r, r, False)
                        norms(o + r - 1, 1 - r, False)
                        proj_out(o + r - 2, r, False)
                norms(NO - 1, 1, False)
                proj_out(NO - 2, 0, False)
                proj_out(NO - 1, 1, False)
            if stop >= 5:
                ffn(1)

        @block.scalar
        def _(act):
            a = nc.scalar.activation
            steps = Steps(act, sem("act_steps"))

            def take_weights():
                for n in range(NWT):
                    act.wait_ge(w_turned, n + 1)
                    if n < 3 * KT:
                        a(cw[:, n, :], ps[n % 4][:, 0:P], ACT.Copy).then_inc(w_taken, 1)
                    elif n < NWT - 1:
                        a(gw[:, n - 3 * KT, :], ps[n % 4][:, 0:P], ACT.Copy).then_inc(w_taken, 1)
                    else:
                        act.wait_ge(w_in, 16 * (6 + 3 * H + 1 + 2 * H))
                        a(wo[:, :], ps[n % 4][:, 0:P], ACT.Identity, scale=onw[:, 0:1]).then_inc(w_taken, 1)

            def root(n):
                act.wait_ge(sem(f"var_ready{n}"), 1)
                a(rstd[:, :], var[:, :], ACT.Sqrt, bias=ceps[:, 0:1]).then_inc(sem(f"std_ready{n}"), 1)

            def ffn(k):
                s = ffn_sems(k)
                root(k)

                def take(g):
                    act.wait_ge(s["xn_turned"], g + 1)
                    if not isinstance(g, int):
                        act.wait_ge(s["logits_done"], g)
                    a(YT4.rearrange("p t d -> p (t d)"), ps[4][:, :], ACT.Copy).then_inc(s["xnT_taken"], 1)
                take(0)
                with act.Fori(1, NG) as g:
                    take(g)
                act.wait_ge(s["z_ready"], 1)
                a(ex, ex, ACT.Exp).then_inc(s["exp_ready"], 1)

                def expert(j, r):
                    e = j * 2 + r
                    act.wait_ge(s["rows_used"], e + 1)
                    a(XET[:, r, :], ps[r][:, :], ACT.Copy).then_inc(s["rowsT_ready"], 1)
                    act.wait_ge(s["w1_used"], e + 1)
                    if not isinstance(j, int):
                        act.wait_ge(s["eout_done"], e - 1)
                    a(HT[:, r, :], ps[2 + r][:, :], ACT.Relu, bias=B1[:, ds(e, 1)]).then_inc(s["hidden_ready"], 1)
                expert(0, 0)
                expert(0, 1)
                with act.Fori(1, E // 2) as j:
                    for r in range(2):
                        expert(j, r)

            take_weights()
            if stop >= 1:
                ffn(0)
            if stop >= 2:
                root("_a")

                def take(g):
                    act.wait_ge(sem("xn_turned_a"), g + 1)
                    b, l = g // (NG // B), g % (NG // B)
                    a(XNT[:, b, ds(l * 512 + KT - 1, 512)], ps[4][:, :], ACT.Copy).then_inc(sem("xnT_taken_a"), 1)
                for b in range(B):
                    with act.Fori(0, NG // B) as l:
                        act.wait_ge(sem("xn_turned_a"), l + (NG // B) * b + 1)
                        a(XNT[:, b, ds(l * 512 + KT - 1, 512)], ps[4][:, :], ACT.Copy).then_inc(sem("xnT_taken_a"), 1)

                def span(s, first):
                    for n in range(12):
                        kind, b = n // 2, n % 2
                        act.wait_ge(sem("proj_done"), s * 12 + n + 1)
                        if not first:
                            if n == 0:
                                act.wait_ge(sem("q_free"), s)
                            if n == 2:
                                act.wait_ge(sem("k_free"), s)
                            if n == 4:
                                act.wait_ge(sem("v_free"), s)
                        src = ps[n % 4][:, :]
                        if kind < 3:
                            a((qT, kT, vT)[kind][:, b, :], src, ACT.Silu).then_inc(sem("silu_ready"), 1)
                            act.wait_ge(sem("silu_ready"), s * 6 + n + 1)
                        elif kind == 3:
                            a(ga[:, b, :], src, ACT.Sigmoid).then_inc(sem("gates_ready"), 1)
                            a(gb[:, b, :], src, ACT.Sigmoid, scale=-1.0).then_inc(sem("gates_ready"), 1)
                            act.wait_ge(sem("gates_ready"), s * 8 + 2 * b + 2)
                        elif kind == 4:
                            if not first and b == 0:
                                act.wait_ge(sem("be_free"), s)
                            a(be[:, b, :], src, ACT.Sigmoid).then_inc(sem("gates_ready"), 1)
                            act.wait_ge(sem("gates_ready"), s * 8 + 5 + b)
                        else:
                            a(MX[:, b, ds(s * 512, 512)], src, ACT.Sigmoid, bias=mbias[:, 0:1]).then_inc(sem("gates_ready"), 1)
                            act.wait_ge(sem("gates_ready"), s * 8 + 7 + b)
                        act.sem_inc(sem("proj_free"), 1)
                span(0, True)
                with act.Fori(1, SG) as i:
                    span(i, False)

            if stop >= 3:
                act.wait_ge(sem("uw_cleared"), 1)

                def spread(o, first):
                    for half in range(2):
                        act.wait_ge(sem("wu_done"), 2 * o + half + 1)
                        if not first and half == 0:
                            act.wait_ge(sem("mqbo_done"), o)
                        for dst, c0 in ((BDU, 0), (BDW, CH)):
                            for h in range(H):
                                q = slice(CH * h, CH * h + CH)
                                last = a(dst[q, 4 * half:4 * half + 4, h, :],
                                         ps[half][q, 0:256].rearrange("p (c x) -> p c x", c=4)[:, :, c0:c0 + CH], ACT.Copy)
                                steps_uw.did(last)
                        steps_uw.wait()
                        act.sem_inc(sem("uw_taken"), 1)

                steps_uw = Steps(act, sem("uw_steps"))
                spread(0, True)
                with act.Fori(1, NO) as o:
                    steps_uw.enter(o, 1, 16)
                    spread(o, False)
                steps_uw.leave(NO - 1)

            if stop >= 4:
                def square(o, r, first):
                    act.wait_ge(sem("o_ready"), o + 1)
                    if not first:
                        act.wait_ge(sem("oss_done"), o - 1)
                    a(osq[r], o3[r], ACT.Square).then_inc(sem("osq_ready"), 1)

                def rms(o, r):
                    act.wait_ge(sem("oss_done"), o + 1)
                    if not (isinstance(o, int) and o < 2):
                        act.wait_ge(sem("on_ready"), o - 1)
                    a(ors[r].rearrange("p b x -> p (b x)"), ps[2 + r][:, 0:256], ACT.Sqrt, bias=ceps[:, 1:2],
                      scale=1.0 / CH).then_inc(sem("ors_ready"), 1)
                square(0, 0, True)
                square(1, 1, True)
                rms(0, 0)
                square(2, 0, False)
                rms(1, 1)
                with act.Fori(1, (NO - 1) // 2) as j:
                    o = j * 2 + 1
                    for r in range(2):
                        square(o + r, 1 - r, False)
                        rms(o + r - 1, r)
                square(NO - 1, 1, False)
                rms(NO - 2, 0)
                rms(NO - 1, 1)
            if stop >= 5:
                ffn(1)

        @block.vector
        def _(dve):
            v = nc.vector
            st_ = Steps(dve, sem("dve_steps"))
            did = lambda i: st_.did(i)

            did(v.memset(XG[:, :, :], 0.0))
            st_.wait()
            dve.sem_inc(zero_ready, 1)
            dve.wait_ge(w_in, 16 * (6 + 3 * H + 1 + 2 * H))
            for n in range(3 * KT):
                v.tensor_scalar(wsc[n], wraw[:, n // KT, :], craw[:, n // KT, n % KT:n % KT + 1], None, ALU.mult).then_inc(w_scaled, 1)

            def all_means(n):
                with dve.Fori(0, NG) as g:
                    st_.enter(g, 0, TG)
                    for k in range(TG):
                        did(v.bn_stats(st[:, ds(g * TG + k, 1), :].rearrange("p t x -> p (t x)"),
                                       X[:, ds(g * TG + k, 1), :].rearrange("p t d -> p (t d)")))
                st_.leave(NG)
                st_.wait()
                did(v.tensor_tensor(mean[:, :], st[:, :, 1], st[:, :, 4], ALU.subtract))
                did(v.tensor_tensor(var[:, :], st[:, :, 2], st[:, :, 5], ALU.add))
                st_.wait()
                did(v.scalar_tensor_tensor(out=rstd[:, :], in0=mean[:, :], scalar=0.25, in1=mean[:, :], op0=ALU.mult, op1=ALU.mult))
                st_.wait()
                did(v.tensor_tensor(mean[:, :], st[:, :, 1], st[:, :, 4], ALU.add))
                st_.wait()
                v.scalar_tensor_tensor(out=var[:, :], in0=var[:, :], scalar=1.0 / D, in1=rstd[:, :], op0=ALU.mult,
                                       op1=ALU.add).then_inc(sem(f"var_ready{n}"), 1)
                did(v.tensor_scalar(mean[:, :], mean[:, :], 0.5, None, ALU.mult))
                st_.wait()

            def invert(n):
                dve.wait_ge(sem(f"std_ready{n}"), 1)
                did(v.reciprocal(rstd[:, :], rstd[:, :]))
                st_.wait()

            def normalise(n):
                def body(g, first):
                    if not first:
                        dve.wait_ge(sem(f"xn_turned{n}"), g)
                    for k in range(TG):
                        t1 = g * TG + k
                        v.tensor_scalar(XN4[:, k, :], X[:, ds(t1, 1), :].rearrange("p t d -> p (t d)"), mean[:, ds(t1, 1)],
                                        rstd[:, ds(t1, 1)], ALU.subtract, ALU.mult).then_inc(sem(f"xn_ready{n}"), 1)
                body(0, True)
                with dve.Fori(1, NG) as g:
                    body(g, False)

            def ffn(k):
                s = ffn_sems(k)
                all_means(k)
                invert(k)
                normalise(k)
                dve.wait_ge(fw_in, 16 * 5 * (k + 1))
                dve.wait_ge(consts, k + 1)
                bce = lambda a: a.unsqueeze(2).to_broadcast([P, NT, E])
                bct = lambda a: a.unsqueeze(1).to_broadcast([P, NT, E])
                dve.wait_ge(s["logits_done"], NG)
                did(v.tensor_tensor(lg, ps[5][:, 0:NT * E].rearrange("p (t e) -> p t e", e=E), bct(brb), ALU.add))
                st_.wait()
                did(v.tensor_reduce(mx, lg, AX_X, ALU.max))
                st_.wait()
                v.tensor_tensor(ex, lg, bce(mx), ALU.subtract).then_inc(s["z_ready"], 1)
                did(v.tensor_tensor(eq, lg, bce(mx), ALU.is_equal))
                st_.wait()
                did(v.tensor_tensor(eq, eq, bct(rev), ALU.mult))
                st_.wait()
                did(v.tensor_reduce(mrev, eq, AX_X, ALU.max))
                st_.wait()
                v.tensor_tensor(oh, bct(rev), bce(mrev), ALU.is_equal).then_inc(s["onehot_ready"], 1)
                dve.wait_ge(s["exp_ready"], 1)
                did(v.tensor_reduce(sm, ex, AX_X, ALU.add))
                st_.wait()
                did(v.reciprocal(gate, sm))
                dve.wait_ge(s["ranks_done"], 1)
                did(v.tensor_copy(eview(tot), ps[7][:, 0:NT * E].rearrange("p (t e) -> p t e", e=E)))
                st_.wait()
                did(v.tensor_tensor_scan(incl, rmask, tot, 0.0, ALU.mult, ALU.add))
                st_.wait()
                did(v.tensor_tensor(incl, incl, tot, ALU.subtract))
                st_.wait()
                did(v.tensor_tensor(incl, incl, eoff, ALU.add))
                st_.wait()
                did(v.tensor_tensor(cum, ps[6][:, 0:NT * E].rearrange("p (t e) -> p t e", e=E), eview(incl), ALU.add))
                st_.wait()
                did(v.tensor_tensor(cum, cum, oh, ALU.mult))
                st_.wait()
                did(v.tensor_reduce(slot, cum, AX_X, ALU.add))
                st_.wait()
                did(v.scalar_tensor_tensor(out=tmp1, in0=mrev, scalar=float(CAP), in1=slot, op0=ALU.mult, op1=ALU.add))
                st_.wait()
                did(v.tensor_scalar(keep, tmp1, float(CAP * E + CAP), None, ALU.is_lt))
                st_.wait()
                did(v.tensor_tensor(gate, gate, keep, ALU.mult))
                did(v.tensor_tensor(gidx, slot, keep, ALU.mult))
                did(v.tensor_tensor(tmp1, slot, trash, ALU.subtract))
                st_.wait()
                did(v.tensor_tensor(tmp1, tmp1, keep, ALU.mult))
                did(v.tensor_scalar(hgate, gate, 0.5, None, ALU.mult))
                did(v.tensor_tensor(rstd[:, :], rstd[:, :], gate, ALU.mult))
                st_.wait()
                did(v.tensor_tensor(sidx, tmp1, trash, ALU.add))
                st_.wait()
                if k == 0:
                    dve.wait_ge(zeroed, 16 * E)
                with dve.Fori(0, NG) as g:
                    for j in range(TG):
                        t1 = g * TG + j
                        v.tensor_scalar(XG[:, ds(t1, 1), :].rearrange("p t d -> p (t d)"), X[:, ds(t1, 1), :].rearrange("p t d -> p (t d)"),
                                        mean[:, ds(t1, 1)], rstd[:, ds(t1, 1)], ALU.subtract, ALU.mult).then_inc(s["rows_ready"], 1)

                def expert(j, r):
                    e = j * 2 + r
                    dve.wait_ge(s["eout_done"], e + 1)
                    if not isinstance(j, int):
                        dve.wait_ge(s["stored"][r], j * 16)
                    v.tensor_tensor(EO[:, r], ps[4 + r][:, :].rearrange("p (s d) -> p s d", s=4),
                                    B2[:, ds(e, 1), :].to_broadcast([P, 4, D]), ALU.add).then_inc(s["eout_ready"], 1)
                expert(0, 0)
                expert(0, 1)
                with dve.Fori(1, E // 2) as j:
                    for r in range(2):
                        expert(j, r)
                for g in range(NG):
                    dve.wait_ge(sem(f"gathered{k}_{g}"), 16 * TG)
                    for j in range(TG):
                        n = g * TG + j
                        v.scalar_tensor_tensor(out=X[:, n, :], in0=XG[:, n, :], scalar=hgate[:, n:n + 1], in1=X[:, n, :],
                                               op0=ALU.mult, op1=ALU.add).then_inc(sem(f"added{k}"), 1)
                dve.wait_ge(sem(f"added{k}"), NT)

            dve.wait_ge(x_in, 32)
            if stop >= 1:
                ffn(0)

            if stop >= 2:
                all_means("_a")
                invert("_a")
                normalise("_a")

                turned = lambda a: a.rearrange("p b (q x) -> p q b x", x=P)
                row = lambda a: a.rearrange("p m d -> p (m d)")

                def span(s, first):
                    dve.wait_ge(sem("silu_ready"), 6 * s + 2)
                    v.transpose(row(qC), turned(qT)).then_inc(sem("qk_chunked"), 1)
                    dve.wait_ge(sem("silu_ready"), 6 * s + 4)
                    v.transpose(row(kC), turned(kT)).then_inc(sem("qk_chunked"), 1)
                    dve.wait_ge(sem("qk_chunked"), 2 * s + 2)
                    dve.sem_inc(sem("q_free"), 1)
                    dve.sem_inc(sem("k_free"), 1)
                    dve.wait_ge(sem("silu_ready"), 6 * s + 6)
                    did(v.transpose(row(vC), turned(vT)))
                    dve.wait_ge(sem("gates_ready"), 8 * s + 6)
                    did(v.transpose(row(bC), turned(be)))
                    st_.wait()
                    dve.sem_inc(sem("be_free"), 1)
                    did(v.tensor_copy(VKA[:, ds(s * M, M), 0:CH], vC))
                    did(v.tensor_scalar(nb[:, :], bC[:, :, 0], -1.0, None, ALU.mult))
                    dve.wait_ge(sem("sq_ready"), 2 * s + 1)
                    did(v.tensor_reduce(rn[:, 0, :], sqq, AX_X, ALU.add))
                    dve.wait_ge(sem("sq_ready"), 2 * s + 2)
                    did(v.tensor_reduce(rn[:, 1, :], sqk, AX_X, ALU.add))
                    st_.wait()
                    v.tensor_scalar(rn[:, :, :], rn[:, :, :], EPS_L2, None, ALU.add).then_inc(sem("ss_ready"), 1)
                    dve.wait_ge(sem("gv_ready"), s + 1)
                    for b in range(B):
                        did(v.tensor_tensor_scan(EM[:, b, ds(s * 512, 512)], ga[:, b, :], gb[:, b, :],
                                                 0.0 if first else EM[:, b, ds(s * 512 - 1, 1)], ALU.mult, ALU.add))
                    st_.wait()
                    dve.sem_inc(sem("v_free"), 1)
                    dve.wait_ge(sem("rn_ready"), s + 1)
                    did(v.tensor_tensor(qC, qC, rn[:, 0, :].unsqueeze(2).to_broadcast([P, M, CH]), ALU.mult))
                    did(v.tensor_tensor(kC, kC, rn[:, 1, :].unsqueeze(2).to_broadcast([P, M, CH]), ALU.mult))
                    st_.wait()
                    did(v.transpose(KQ[:, :, CH:64], qC))
                    did(v.transpose(KQ[:, :, 0:CH], kC))
                    did(v.tensor_copy(VKA[:, ds(s * M, M), CH:64], kC))
                    st_.wait()
                    dve.sem_inc(sem("kq_ready"), 1)
                    did(v.tensor_copy(QN[:, ds(s * M, M), :], KQ[:, :, CH:64]))
                    for n in range(M // 8):
                        dve.wait_ge(sem("gram_half"), 8 * s + 2 * n + 2)
                        pv = ps[4 + n % 2][:, :].rearrange("p (c x) -> p c x", x=64)
                        did(v.tensor_tensor(AG[:, 8 * n:8 * n + 8, :], pv[:, :, 0:CH],
                                            nb[:, 8 * n:8 * n + 8].unsqueeze(2).to_broadcast([P, 8, CH]), ALU.mult))
                        did(v.tensor_tensor(VKA[:, ds(s * M + 8 * n, 8), 64:96], pv[:, :, CH:64],
                                            triu[:, :].unsqueeze(1).to_broadcast([P, 8, CH]), ALU.mult))
                        st_.wait()
                        dve.sem_inc(sem("gram_taken"), 1)
                    did(v.transpose(RA, AG.rearrange("p m j -> p j m")))
                    did(v.memset(row(RT), 0.0))
                    st_.wait()
                    did(v.memset(row(RT)[:, 0:CH * CH:CH + 1], 1.0))
                    st_.wait()
                    for j in range(CH - 1):
                        n = CH - 1 - j
                        pr = prod_view(n, j + 1)
                        did(v.tensor_tensor(pr, RA[:, j, j + 1:CH].unsqueeze(2).to_broadcast([P, n, j + 1]),
                                            RT[:, j:j + 1, 0:j + 1].to_broadcast([P, n, j + 1]), ALU.mult))
                        st_.wait()
                        did(v.tensor_tensor(RT[:, j + 1:CH, 0:j + 1], RT[:, j + 1:CH, 0:j + 1], pr, ALU.add))
                        st_.wait()
                    did(v.transpose(TC.rearrange("p m i -> p i m"), RT))
                    st_.wait()
                    did(v.tensor_tensor(TT[:, ds(s * 1024, 1024)].rearrange("p (m d) -> p m d", d=CH), TC,
                                        bC[:, :, 0:1].to_broadcast([P, M, CH]), ALU.mult))
                    st_.wait()
                    dve.sem_inc(sem("tt_ready"), 1)

                def prod_view(n, w):
                    return prod[:, 0:n * w].rearrange("p (i c) -> p i c", c=w)
                PER = 2 + 2 + 2 + 2 + 2 + 3 + 1 + 2 * (M // 8) + 3 + 2 * (CH - 1) + 2
                span(0, True)
                with dve.Fori(1, SG) as i:
                    st_.enter(i, 1, PER)
                    span(i, False)
                st_.leave(SG - 1)

            if stop >= 3:
                did(v.memset(W[1][:, :], 0.0))
                did(v.memset(W[2][:, :], 0.0))
                did(v.memset(Sst[:, :], 0.0))
                st_.wait()
                dve.sem_inc(sem("uw_cleared"), 2)
                dve.sem_inc(sem("state_done"), 1)

                def take(o):
                    dve.wait_ge(sem("mqbo_done"), o + 1)
                    pm = ps[2][:, :].rearrange("p (c x) -> p c x", x=64)
                    pb = ps[3][:, :].rearrange("p (c x) -> p c x", x=64)
                    did(v.tensor_tensor(BDP, pm[:, :, 0:CH].unsqueeze(2).to_broadcast([P, 8, H, CH]),
                                        negbd[:, :, :].unsqueeze(1).to_broadcast([P, 8, H, CH]), ALU.mult))
                    did(v.transpose(Bc, pb[:, :, 0:CH]))
                    did(v.tensor_tensor(QN[:, ds(o * 8, 8), :], QN[:, ds(o * 8, 8), :], pm[:, :, CH:64], ALU.subtract))
                    did(v.tensor_copy(VKA[:, ds(o * 8, 8), 0:CH], pb[:, :, CH:64]))
                    st_.wait()
                    dve.sem_inc(sem("mq_taken"), 1)

                def chain(o):
                    for k in range(4):
                        Sv = Sst[:, :].rearrange("p (b d) -> p b d", b=B)
                        did(v.tensor_copy(VKA[:, ds(o * 8 + k, 5), CH:64][:, 0:5:4, :], Sv))
                        did(v.tensor_tensor(SBs[:, :].rearrange("p (b d) -> p b d", b=B), Sv, Bc[:, k:8:4, :], ALU.add))
                        st_.wait()
                        dve.wait_ge(sem("chain_done"), o * 4 + k + 1)
                        v.tensor_tensor(Sst[:, :], ps[4 + k % 2][:, 0:B * CH], SBs[:, :], ALU.add).then_inc(sem("state_done"), 1)
                        dve.wait_ge(sem("state_done"), o * 4 + k + 2)
                take(0)
                with dve.Fori(1, NO) as o:
                    st_.enter(o, 1, 12)
                    chain(o - 1)
                    take(o)
                st_.leave(NO - 1)
                chain(NO - 1)

            if stop >= 4:
                def delta(o, r):
                    dve.wait_ge(sem("od_done"), o + 1)
                    if not (isinstance(o, int) and o < 2):
                        dve.wait_ge(sem("mix_ready"), o - 1)
                    v.tensor_tensor(o1[r].rearrange("p b (c d) -> p (b c) d", d=CH), ps[r][:, 0:256].rearrange("p (c d) -> p c d", d=CH),
                                    VKA[:, ds(o * 8, 8), 0:CH], ALU.add).then_inc(sem("od_ready"), 1)

                def mixed(o, r):
                    dve.wait_ge(sem("mix_ready"), o + 1)
                    dve.wait_ge(sem("od_ready"), o + 1)
                    if not (isinstance(o, int) and o < 2):
                        dve.wait_ge(sem("osq_ready"), o - 1)
                        dve.wait_ge(sem("on_ready"), o - 1)
                    v.tensor_tensor(o3[r], o1[r], o2[r], ALU.add).then_inc(sem("o_ready"), 1)

                def scaled(o, r):
                    dve.wait_ge(sem("ors_ready"), o + 1)
                    dve.wait_ge(sem("o_ready"), o + 1)
                    did(v.reciprocal(ors[r], ors[r]))
                    st_.wait()
                    if not (isinstance(o, int) and o < 2):
                        dve.wait_ge(sem("wo_done"), o - 1)
                    v.tensor_tensor(on[r], o3[r], ors[r], ALU.mult).then_inc(sem("on_ready"), 1)

                def residual(o, r):
                    dve.wait_ge(sem("wo_done"), o + 1)
                    xo = X[:, :, :].rearrange("p (b t) d -> p b t d", b=B)[:, :, ds(o, 1), :].rearrange("p b t d -> p b (t d)")
                    v.tensor_tensor(xo, xo, ps[6 + r][:, 0:256].rearrange("p (b d) -> p b d", b=B),
                                    ALU.add).then_inc(sem("attn_added"), 1)
                delta(0, 0)
                delta(1, 1)
                mixed(0, 0)
                delta(2, 0)
                mixed(1, 1)
                scaled(0, 0)
                delta(3, 1)
                mixed(2, 0)
                scaled(1, 1)
                residual(0, 0)
                with dve.Fori((4) // 2, (NO) // 2) as j:
                    o = j * 2
                    st_.enter(j, 2, 2)
                    for r in range(2):
                        delta(o + r, r)
                        mixed(o + r - 1, 1 - r)
                        scaled(o + r - 2, r)
                        residual(o + r - 3, 1 - r)
                st_.leave((NO - 4) // 2)
                mixed(NO - 1, 1)
                scaled(NO - 2, 0)
                residual(NO - 3, 1)
                scaled(NO - 1, 1)
                residual(NO - 2, 0)
                residual(NO - 1, 1)
                dve.wait_ge(sem("attn_added"), NO)
                dve.sem_inc(sem("attn_done"), 1)
            if stop >= 5:
                ffn(1)
            if dump is not None:
                dve.drain().then_inc(sem("fin"), 1)


_INS = ["L0_attn_hidden_states", "L0_attn_Wq", "L0_attn_Wk", "L0_attn_Wv", "L0_attn_Wb", "L0_attn_Wdec",
        "L0_attn_Wmix", "L0_attn_mix_bias", "L0_attn_wq_conv", "L0_attn_wk_conv", "L0_attn_wv_conv",
        "L0_attn_onorm_w", "L0_attn_Wo", "L0_ffn_Wr", "L0_ffn_br", "L0_ffn_W1", "L0_ffn_b1", "L0_ffn_W2",
        "L0_ffn_b2"]


def kernel(**inputs):
    import numpy as _np
    import concourse.bacc as _bacc
    from concourse import mybir as _mybir
    from concourse.bass_utils import run_bass_kernel_spmd as _run

    nc = _bacc.Bacc("TRN2", target_bir_lowering=False, num_devices=1)
    arrays, tensors = {}, {}
    for name in _INS:
        a = _np.ascontiguousarray(inputs[name])
        arrays[f"in_{name}"] = a
        tensors[name] = nc.dram_tensor(f"in_{name}", a.shape, _mybir.dt.from_np(a.dtype), kind="ExternalInput").ap()
    shape = tuple(inputs["L0_attn_hidden_states"].shape)
    out = nc.dram_tensor("out_x", shape, _mybir.dt.from_np(_np.dtype("float32")), kind="ExternalOutput").ap()
    macaron_kernel(nc, tensors, out)
    r = _run(nc, [arrays], core_ids=[0])
    return r.results[0]["out_x"]
```

```python
import concourse.bass as bass
from concourse import mybir
from contextlib import ExitStack

F32 = mybir.dt.float32
BF16 = mybir.dt.bfloat16
U32 = mybir.dt.uint32
ALU = mybir.AluOpType
ACT = mybir.ActivationFunctionType
AX_X = mybir.AxisListType.X
ds = bass.ds

P = 128
CH = 32
EPS_LN = 1e-5
EPS_L2 = 1e-6
EPS_RMS = 1e-5


class Steps:

    def __init__(self, eng, sem):
        self.eng, self.sem = eng, sem
        self.base, self.local, self.reg, self.per = 0, 0, None, 0

    def did(self, instruction):
        instruction.then_inc(self.sem, 1)
        self.local += 1
        return instruction

    def value(self, back=0):
        v = self.base + self.local - back
        return v if self.reg is None else (self.reg - self.first) * (self.per // self.step) + v

    def wait(self, back=0):
        self.eng.wait_ge(self.sem, self.value(back))

    def enter(self, reg, first, per, step=1):
        assert per % step == 0
        self.base += self.local
        self.reg, self.first, self.per, self.step, self.local = reg, first, per, step, 0

    def leave(self, times):
        assert self.local == self.per, (self.local, self.per)
        self.base += self.per * times
        self.reg, self.local = None, 0


def macaron_kernel(nc, t, out, stop=99, dump=None):
    x_d = t["L0_attn_hidden_states"]
    B, L, D = x_d.shape
    H = t["L0_attn_Wb"].shape[0]
    KT = t["L0_attn_wq_conv"].shape[1]
    E = t["L0_ffn_Wr"].shape[1]
    N = B * L
    CAP = N // E
    NT = N // P
    TG = 4
    NG = NT // TG
    SG = L // 512
    NO = L // P
    M = 2 * 512 // CH
    R = H * CH
    assert (B, D, H * CH, CAP, R, M) == (2, P, P, 512, P, 32)

    x_v = x_d.rearrange("b (t p) d -> p (b t) d", p=P)
    out_v = out.rearrange("b (t p) d -> p (b t) d", p=P)
    slots_d = nc.dram_tensor("expert_rows", [2 * N, D], F32).ap()
    eout_d = nc.dram_tensor("expert_out", [N, D], F32).ap()
    slots_v = slots_d[0:N, :].rearrange("(e p s) d -> e p (s d)", p=P, s=CAP // P)
    eout_v = eout_d.rearrange("(e p s) d -> e p (s d)", p=P, s=CAP // P)

    ctx = ExitStack()
    with ctx:
        def sb(name, shape, dt=F32):
            return ctx.enter_context(nc.sbuf_tensor(name, shape, dt))

        sems = {}

        def sem(name):
            if name not in sems:
                sems[name] = ctx.enter_context(nc.semaphore(name))
            return sems[name]

        ps = [ctx.enter_context(nc.psum_tensor(f"bank{i}", [P, 512], F32)) for i in range(8)]

        X = sb("X", [P, NT, D])
        XG = sb("XG", [P, NT, D])
        XNT = sb("XNT", [P, B, L + KT - 1])
        VKA = sb("VKA", [P, NO * 8, 96])
        QN = sb("QN", [P, NO * 8, CH])
        EM = sb("EM", [P, B, L])
        MX = sb("MX", [P, B, L])
        W = [sb(f"W{i}", [P, 1024]) for i in range(11)]
        KQ = sb("KQ", [P, M, 64])
        TT = XG[:, :, :].rearrange("p t d -> p (t d)")

        ident = sb("ident", [P, P])
        bdm = sb("bdm", [P, H, CH])
        triu = sb("triu", [P, CH])
        cw = sb("cw", [P, 3 * KT, P])
        gw = sb("gw", [P, 3, P])
        wo = sb("wo", [P, P])
        mbias = sb("mbias", [P, 1])
        onw = sb("onw", [P, 1])
        ceps = sb("ceps", [P, 3])
        mean = sb("mean", [P, NT])
        var = sb("var", [P, NT])
        rstd = sb("rstd", [P, NT])
        rn = sb("rn", [P, 2, M])
        beta = sb("beta", [P, NO * 8])
        nbeta = sb("nbeta", [P, NO * 8])

        arena = VKA[:, :, :].rearrange("p m c -> p (m c)")
        used = [0]

        def part(n):
            used[0] += n
            assert used[0] <= NO * 8 * 96
            return arena[:, used[0] - n:used[0]]

        XE = part(2 * 512).rearrange("p (r s d) -> p r s d", r=2, s=4)
        EO = part(2 * 512).rearrange("p (r s d) -> p r s d", r=2, s=4)
        HT = part(2 * 512).rearrange("p (r n) -> p r n", r=2)
        XET = part(2 * 512).rearrange("p (r n) -> p r n", r=2)
        W1 = part(2 * 128).rearrange("p (r n) -> p r n", r=2)
        W2 = part(E * D).rearrange("p (e n) -> p e n", e=E)
        B2 = part(E * D).rearrange("p (e n) -> p e n", e=E)
        B1 = part(E)
        wr = part(E)
        brb = part(E)
        st = part(NT * 6).rearrange("p (t x) -> p t x", x=6)
        XN = part(2 * TG * D).rearrange("p (r t d) -> p r t d", r=2, t=TG)
        YT = part(2 * TG * D).rearrange("p (r t d) -> p r t d", r=2, t=TG)
        te = lambda: part(NT * E).rearrange("p (t e) -> p t e", e=E)
        lg, eq, ex, cum = te(), te(), te(), te()
        tot, incl, rmask, eoff = part(NT * E), part(NT * E), part(NT * E), part(NT * E)
        mx, sm, gate, keep, hgate, slot, trash, tmp1, mrev = [part(NT) for _ in range(9)]
        rev = part(E)
        sidx = part(NT).bitcast(U32)
        gidx = part(NT).bitcast(U32)
        i1 = part(NT * E).bitcast(mybir.dt.int32)
        oh = part(NT * E // 2).bitcast(BF16).rearrange("p (t e) -> p t e", e=E)
        tri = part(P // 2).bitcast(BF16)
        onesb = part(P // 2).bitcast(BF16)

        def eview(a):
            return a.rearrange("p (e t) -> p t e", e=E)

        def bt(i):
            return W[i][:, :].rearrange("p (b l) -> p b l", b=B)
        qT, kT, vT, ga, gb, be = [bt(i) for i in range(6)]
        qC, kC, vC, bC = [W[i][:, :].rearrange("p (m d) -> p m d", d=CH) for i in (6, 7, 8, 9)]
        sqq = W[10][:, :].rearrange("p (m d) -> p m d", d=CH)
        sqk = KQ[:, 0:M // 2, :].rearrange("p m d -> p (m d)").rearrange("p (m d) -> p m d", d=CH)
        AG = qC
        TC = qC
        RA = W[10][:, :].rearrange("p (j i) -> p j i", j=CH)
        RT = W[9][:, :].rearrange("p (i c) -> p i c", c=CH)
        prod = [W[6][:, 0:512], W[6][:, 512:1024]]

        pairs = [W[w][:, 512 * k:512 * k + 512] for w in range(10) for k in range(2)]
        chunks = lambda a, n=CH: a.rearrange("p (c d) -> p c d", d=n)
        VKAs = [W[0][:, 0:768], W[1][:, 0:768]]
        TTs = [W[0][:, 768:1024], W[1][:, 768:1024]]
        VKAs = [chunks(a, 96) for a in VKAs]
        TTs = [chunks(a) for a in TTs]
        ring = lambda n: [pairs[n][:, 0:256], pairs[n][:, 256:512]]
        UWs = [chunks(pairs[4], 64), chunks(pairs[5], 64)]
        PTs = [chunks(a) for a in ring(6)]
        BTs = [chunks(a) for a in ring(7)]
        QTs = [chunks(a) for a in ring(8)]
        OIs = ring(9)
        Sh = [a.rearrange("p (k b d) -> p k b d", k=4, b=B) for a in ring(10)]
        od = ring(11)
        dm = ring(12)
        om = ring(13)
        osq = ring(14)
        ors = ring(15)
        on = ring(16)
        SBs = pairs[17][:, 0:B * CH]
        both = lambda a: a.rearrange("p (b x) -> p b x", b=B)

        def ffn_sems(k):
            return {n: sem(f"{n}{k}") for n in (
                "mean_steps", "var_ready", "std_ready", "xn_ready", "xn_turned", "xnT_taken",
                "logits_done", "z_ready", "exp_ready", "onehot_ready", "ranks_done", "rows_ready",
                "scattered", "w1_used", "rows_used", "rows_turned", "rowsT_ready", "hidden_done",
                "hidden_ready", "eout_done", "eout_ready", "added")} | {
                n: [sem(f"{n}{k}_{r}") for r in range(2)] for n in ("w1_in", "rows_in", "stored")}

        XQ = 4
        w_in = sem("w_in")
        fw_in = sem("fw_in")
        zero_ready = sem("zero_ready")
        zeroed = sem("zeroed")
        consts = sem("consts")
        w_scaled = sem("w_scaled")
        w_turned = sem("w_turned")
        w_taken = sem("w_taken")
        NWT = 3 * KT + 4

        block = ctx.enter_context(nc.Block())

        wsrc = [(t["L0_attn_Wq"], t["L0_attn_wq_conv"]), (t["L0_attn_Wk"], t["L0_attn_wk_conv"]),
                (t["L0_attn_Wv"], t["L0_attn_wv_conv"])]
        wraw = W[0][:, 0:3 * P].rearrange("p (n d) -> p n d", n=3)
        graw = W[0][:, 3 * P:6 * P].rearrange("p (n d) -> p n d", n=3)
        woraw = W[0][:, 6 * P:7 * P]
        craw = W[0][:, 7 * P:7 * P + 3 * KT].rearrange("p (n j) -> p n j", n=3)
        wsc = [W[1 + n // 8][:, P * (n % 8):P * (n % 8) + P] for n in range(3 * KT)]

        def runs(i, lag):
            return not isinstance(i, int) or 0 <= i - lag < NO

        locals_ = locals()
        @block.sync
        def _(sp):
            for n in range(XQ):
                q = slice(n * NT // XQ, (n + 1) * NT // XQ)
                sp.dma_start(X[:, q, :], x_v[:, q, :]).then_inc(sem(f"x_in_{n}"), 16)
            with nc.allow_non_contiguous_dma(reason="small"):
                sp.dma_start(wr, t["L0_ffn_Wr"]).then_inc(fw_in, 16)
                sp.dma_start(brb, t["L0_ffn_br"].rearrange("(a e) -> a e", a=1).broadcast_to([P, E])).then_inc(fw_in, 16)
                sp.dma_start(B1, t["L0_ffn_b1"].rearrange("e f -> f e")).then_inc(fw_in, 16)
                sp.dma_start(B2, t["L0_ffn_b2"].rearrange("(a e) d -> a e d", a=1).broadcast_to([P, E, D])).then_inc(fw_in, 16)
                sp.dma_start(W2, t["L0_ffn_W2"].rearrange("e f d -> f e d")).then_inc(fw_in, 16)
            sp.wait_ge(zero_ready, 1)
            for e in range(E):
                sp.dma_start(slots_v[e], XG[:, 4 * e:4 * e + 4, :].rearrange("p s d -> p (s d)")).then_inc(zeroed, 16)
            with nc.allow_non_contiguous_dma(reason="small"):
                for n, (w, c) in enumerate(wsrc):
                    sp.dma_start(wraw[:, n, :], w).then_inc(w_in, 16)
                    sp.dma_start(craw[:, n, :], c).then_inc(w_in, 16)
                for n, w in enumerate(("L0_attn_Wdec", "L0_attn_Wb", "L0_attn_Wmix")):
                    for h in range(H):
                        sp.dma_start(graw[CH * h:CH * h + CH, n, :], t[w][h:h + 1, :].broadcast_to([CH, D])).then_inc(w_in, 16)
                sp.dma_start(woraw, t["L0_attn_Wo"]).then_inc(w_in, 16)
                for h in range(H):
                    sp.dma_start(mbias[CH * h:CH * h + CH, :], t["L0_attn_mix_bias"].rearrange("(h a) -> h a", a=1)[h:h + 1, :].broadcast_to([CH, 1])).then_inc(w_in, 16)
                    sp.dma_start(onw[CH * h:CH * h + CH, :], t["L0_attn_onorm_w"].rearrange("(d a) -> d a", a=1)).then_inc(w_in, 16)
            def ffn_io(k):
                s = ffn_sems(k)

                def load_w1(j, r):
                    if not isinstance(j, int):
                        sp.wait_ge(s["w1_used"], j * 2 + r - 1)
                    sp.dma_start(W1[:, r, :], t["L0_ffn_W1"][ds(j * 2 + r, 1)].rearrange("e d f -> (e d) f")).then_inc(s["w1_in"][r], 16)

                def load_rows(j, r):
                    if not isinstance(j, int):
                        sp.wait_ge(s["rows_used"], j * 2 + r - 1)
                    sp.dma_start(XE[:, r].rearrange("p s d -> p (s d)"),
                                 slots_v[ds(j * 2 + r, 1)].rearrange("e p x -> (e p) x")).then_inc(s["rows_in"][r], 16)

                def store(j, r):
                    e = j * 2 + r
                    sp.wait_ge(s["eout_ready"], e + 1)
                    sp.dma_start(eout_v[ds(e, 1)].rearrange("e p x -> (e p) x"),
                                 EO[:, r].rearrange("p s d -> p (s d)")).then_inc(s["stored"][r], 16)
                if k:
                    sp.wait_ge(sem("attn_done"), 1)
                    for dst, name in ((wr, "L0_ffn_Wr"),):
                        sp.dma_start(dst, t[name]).then_inc(fw_in, 16)
                    with nc.allow_non_contiguous_dma(reason="small"):
                        sp.dma_start(brb, t["L0_ffn_br"].rearrange("(a e) -> a e", a=1).broadcast_to([P, E])).then_inc(fw_in, 16)
                        sp.dma_start(B1, t["L0_ffn_b1"].rearrange("e f -> f e")).then_inc(fw_in, 16)
                        sp.dma_start(B2, t["L0_ffn_b2"].rearrange("(a e) d -> a e d", a=1).broadcast_to([P, E, D])).then_inc(fw_in, 16)
                        sp.dma_start(W2, t["L0_ffn_W2"].rearrange("e f d -> f e d")).then_inc(fw_in, 16)
                load_w1(0, 0)
                load_w1(0, 1)
                sp.wait_ge(s["scattered"], 16 * NT)
                load_rows(0, 0)
                load_rows(0, 1)
                with sp.Fori(0, E // 2 - 1) as j:
                    for r in range(2):
                        load_rows(j + 1, r)
                        load_w1(j + 1, r)
                        store(j, r)
                store(E // 2 - 1, 0)
                store(E // 2 - 1, 1)

            if stop >= 1:
                ffn_io(0)

            if stop >= 4:
                def fetch(o, r):
                    if not (isinstance(o, int) and o < 2):
                        sp.wait_ge(sem("mqbo_done"), o - 1)
                    sp.dma_start(VKAs[r], VKA[:, ds(o * 8, 8), :]).then_inc(sem(f"octet_in_{r}"), 16)
                    sp.dma_start(TTs[r], chunks(TT[:, ds(o * 256, 256)])).then_inc(sem(f"octet_in_{r}"), 16)
                sp.wait_ge(sem("tt_ready"), SG)
                fetch(0, 0)
                fetch(1, 1)
                with sp.Fori(1, NO // 2) as j:
                    fetch(j * 2, 0)
                    fetch(j * 2 + 1, 1)
            if stop >= 5:
                ffn_io(1)
            if dump is not None:
                sp.wait_ge(sem("fin"), 1)
                sp.dma_start(out_v, dump(locals_)).then_inc(sem("out_in"), 16)
                sp.wait_ge(sem("out_in"), 16)
            else:
                with sp.Fori(0, NG) as g:
                    sp.wait_ge(sem("added1"), g * TG + TG)
                    sp.dma_start(out_v[:, ds(g * TG, TG), :], X[:, ds(g * TG, TG), :]).then_inc(sem("out_in"), 16)
                sp.wait_ge(sem("out_in"), 16 * NG)

        @block.gpsimd
        def _(pool):
            g = nc.gpsimd
            sp_ = Steps(pool, sem("pool_steps"))

            def one(instruction):
                sp_.did(instruction)
                sp_.wait()

            def make_consts():
                one(g.memset(ident[:, :], 0.0))
                one(g.memset(bdm[:, :, :], 0.0))
                one(g.memset(triu[:, :], 1.0))
                one(g.memset(ceps[:, 0:1], EPS_LN))
                one(g.memset(ceps[:, 1:2], EPS_RMS))
                one(g.memset(ceps[:, 2:3], EPS_L2))
                one(g.memset(XNT[:, :, 0:KT - 1], 0.0))
                one(g.affine_select(out=ident[:, :], in_=ident[:, :], compare_op=ALU.not_equal, fill=1.0,
                                base=0, pattern=[[-1, P]], channel_multiplier=1))
                for h in range(H):
                    q = slice(CH * h, CH * h + CH)
                    one(g.memset(bdm[q, h, :], 1.0))
                    one(g.affine_select(out=triu[q, :], in_=triu[q, :], compare_op=ALU.is_ge, fill=0.0,
                                    base=0, pattern=[[1, CH]], channel_multiplier=-1))

            def ffn_consts(k):
                one(g.memset(onesb, 1.0))
                one(g.memset(tri, 1.0))
                one(g.memset(rmask, 1.0))
                one(g.affine_select(out=tri, in_=tri, compare_op=ALU.is_ge, fill=0.0, base=0,
                                pattern=[[1, P]], channel_multiplier=-1))
                one(g.memset(rmask.rearrange("p (e t) -> p e t", e=E)[:, :, 0:1], 0.0))
                one(g.iota(i1[:, 0:E], pattern=[[-1, E]], base=E, channel_multiplier=0))
                one(g.tensor_copy(rev, i1[:, 0:E]))
                one(g.iota(i1[:, 0:NT], pattern=[[P, NT]], base=N, channel_multiplier=1))
                one(g.tensor_copy(trash, i1[:, 0:NT]))
                one(g.iota(i1, pattern=[[CAP, E], [0, NT]], base=0, channel_multiplier=0))
                g.tensor_copy(eoff, i1).then_inc(consts, 1)

            make_consts()
            ffn_consts(0)

            def ffn_moves(k):
                s = ffn_sems(k)
                if k == 0:
                    pool.wait_ge(zeroed, 16 * E)
                for n in range(NT):
                    pool.wait_ge(s["rows_ready"], n + 1)
                    g.indirect_dma_start(slots_d, bass.IndirectOffsetOnAxis(ap=sidx[:, n:n + 1], axis=0),
                                         XG[:, n, :], None).then_inc(s["scattered"], 16)
                for r in range(2):
                    pool.wait_ge(s["stored"][r], 16 * (E // 2))
                for n in range(NT):
                    g.indirect_dma_start(XG[:, n, :], None, eout_d,
                                         bass.IndirectOffsetOnAxis(ap=gidx[:, n:n + 1], axis=0)).then_inc(
                                             sem(f"gathered{k}_{n // TG}"), 16)

            if stop >= 1:
                ffn_moves(0)

            def span(s, first):
                pool.wait_ge(sem("silu_ready"), 6 * s + 6)
                pool.wait_ge(sem("gates_ready"), 8 * s + 4)
                g.tensor_tensor(gb, gb, vT, ALU.mult).then_inc(sem("gv_ready"), 1)
                pool.wait_ge(sem("v_chunked"), s + 1)
                g.tensor_copy(VKA[:, ds(s * M, M), 0:CH], vC).then_inc(sem("v_kept"), 1)
                pool.wait_ge(sem("k_normed"), s + 1)
                g.tensor_copy(VKA[:, ds(s * M, M), CH:64], kC).then_inc(sem("k_kept"), 1)
                pool.wait_ge(sem("kq_ready"), 2 * s + 2)
                g.tensor_copy(QN[:, ds(s * M, M), :], KQ[:, :, CH:64]).then_inc(sem("qn_kept"), 1)

            if stop >= 2:
                span(0, True)
                with pool.Fori(1, SG) as i:
                    span(i, False)

            if stop >= 4:
                def mixing(o, r):
                    pool.wait_ge(sem("delta_ready"), o + 1)
                    if not (isinstance(o, int) and o < 2):
                        pool.wait_ge(sem("mixed_ready"), o - 1)
                    g.tensor_tensor(both(dm[r]), EM[:, :, ds(o * P, P)], both(od[r]), ALU.subtract).then_inc(sem("distance_ready"), 1)
                    pool.wait_ge(sem("distance_ready"), o + 1)
                    g.tensor_tensor(both(dm[r]), both(dm[r]), MX[:, :, ds(o * P, P)], ALU.mult).then_inc(sem("gated_ready"), 1)
                mixing(0, 0)
                mixing(1, 1)
                with pool.Fori(1, NO // 2) as j:
                    mixing(j * 2, 0)
                    mixing(j * 2 + 1, 1)
            if stop >= 5:
                pool.wait_ge(sem("attn_done"), 1)
                ffn_consts(1)
                ffn_moves(1)

        @block.tensor
        def _(pe):
            mm = nc.tensor.matmul
            tr = nc.tensor.transpose

            def turn_weights():
                pe.wait_ge(consts, 1)
                for n in range(NWT):
                    pe.wait_ge(w_scaled, min(n + 1, 3 * KT))
                    src = wsc[n] if n < 3 * KT else (graw[:, n - 3 * KT, :] if n < NWT - 1 else woraw)
                    if n >= 4:
                        pe.wait_ge(w_taken, n - 3)
                    tr(ps[n % 4][:, 0:P], src, ident[:, :]).then_inc(w_turned, 1)

            def turn_group(s, g, r):
                pe.wait_ge(s["xn_ready"], g * TG + TG)
                if not (isinstance(g, int) and g < 2):
                    pe.wait_ge(s["xnT_taken"], g - 1)
                for k in range(TG):
                    last = tr(ps[4 + 2 * r][:, P * k:P * k + P], XN[:, r, k, :], ident[:, :])
                last.then_inc(s["xn_turned"], 1)

            def ffn(k):
                s = ffn_sems(k)
                pe.wait_ge(fw_in, 16 * 5 * (k + 1))
                pe.wait_ge(consts, k + 1)

                def logits(g, r):
                    pe.wait_ge(s["xnT_taken"], g + 1)
                    for j in range(TG):
                        last = mm(ps[5][:, ds(g * (TG * E) + j * E, E)], YT[:, r, j, :], wr, start=True, stop=True)
                    last.then_inc(s["logits_done"], 1)
                turn_group(s, 0, 0)
                turn_group(s, 1, 1)
                logits(0, 0)
                with pe.Fori(1, NG // 2) as j:
                    turn_group(s, j * 2, 0)
                    logits(j * 2 - 1, 1)
                    turn_group(s, j * 2 + 1, 1)
                    logits(j * 2, 0)
                logits(NG - 1, 1)
                pe.wait_ge(s["onehot_ready"], 1)
                mm(ps[6][:, 0:NT * E], tri, oh.rearrange("p t e -> p (t e)"), start=True, stop=True)
                mm(ps[7][:, 0:NT * E], onesb, oh.rearrange("p t e -> p (t e)"), start=True, stop=True).then_inc(s["ranks_done"], 1)

                if k == 0:
                    turn_weights()
                    pe.wait_ge(w_taken, NWT)

                def turn_rows(j, r):
                    pe.wait_ge(s["rows_in"][r], j * 16 + 16)
                    for c in range(4):
                        last = tr(ps[r][:, P * c:P * c + P], XE[:, r, c, :], ident[:, :])
                    last.then_inc(s["rows_used"], 1)

                def first_layer(j, r):
                    pe.wait_ge(s["w1_in"][r], j * 16 + 16)
                    pe.wait_ge(s["rowsT_ready"], j * 2 + r + 1)
                    mm(ps[2 + r][:, :], W1[:, r, :], XET[:, r, :], start=True, stop=True).then_inc(s["w1_used"], 1)

                def second_layer(j, r):
                    e = j * 2 + r
                    pe.wait_ge(s["hidden_ready"], e + 1)
                    if not (isinstance(j, int) and j < 1):
                        pe.wait_ge(s["eout_ready"], e - 1)
                    for c in range(4):
                        last = mm(ps[4 + r][:, P * c:P * c + P], HT[:, r, P * c:P * c + P], W2[:, ds(e, 1), :].rearrange("p e d -> p (e d)"),
                                  start=True, stop=True)
                    last.then_inc(s["eout_done"], 1)

                def experts(j, last=False):
                    turn_rows(j, 1)
                    second_layer(j, 0)
                    first_layer(j, 1)
                    if not last:
                        turn_rows(j + 1, 0)
                    second_layer(j, 1)
                    if not last:
                        first_layer(j + 1, 0)
                turn_rows(0, 0)
                first_layer(0, 0)
                experts(0)
                with pe.Fori(1, E // 2 - 1) as j:
                    experts(j)
                experts(E // 2 - 1, True)

            if stop >= 1:
                ffn(0)

            NP = 12

            def project(s, first, part):
                for n in part:
                    kind, b = n // 2, n % 2
                    if not (first and n < 4):
                        pe.wait_ge(sem("proj_free"), s * NP + n - 3)
                    if kind < 3:
                        for j in range(KT):
                            last = mm(ps[n % 4][:, :], cw[:, kind * KT + j, :], XNT[:, b, ds(s * 512 + j, 512)],
                                      start=j == 0, stop=j == KT - 1)
                    else:
                        last = mm(ps[n % 4][:, :], gw[:, kind - 3, :], XNT[:, b, ds(s * 512 + KT - 1, 512)],
                                  start=True, stop=True)
                    last.then_inc(sem("proj_done"), 1)
            conv_part, gate_part = range(0, 6), range(6, NP)
            hs = [slice(CH * h, CH * h + CH) for h in range(H)]

            def passed():
                pe.sem_inc(sem("pe_passed"), 1)

            def gram(s, first):
                pe.wait_ge(sem("kq_ready"), 2 * s + 2)
                for m in range(M):
                    if m % 8 == 0:
                        if not first:
                            pe.wait_ge(sem("gram_taken"), 8 * s + m // 4 - 6)
                        passed()
                    for q in hs:
                        last = mm(ps[4 + m // 8][q, 64 * (m % 8):64 * (m % 8) + 64], KQ[q, m, 0:CH], KQ[q, m, :], start=True, stop=True)
                    if m % 8 == 7:
                        last.then_inc(sem("gram_banks"), 1)

            if stop >= 2:
                s = {n: sem(f"{n}_a") for n in ("xn_ready", "xnT_taken", "xn_turned")}
                turn_group(s, 0, 0)
                turn_group(s, 1, 1)
                with pe.Fori(1, NG // 2) as j:
                    turn_group(s, j * 2, 0)
                    turn_group(s, j * 2 + 1, 1)
                pe.wait_ge(s["xnT_taken"], NG)
                project(0, True, conv_part)
                project(0, True, gate_part)
                project(1, False, conv_part)
                gram(0, True)
                project(1, False, gate_part)
                with pe.Fori(1, SG - 1) as i:
                    project(i + 1, False, conv_part)
                    gram(i, False)
                    project(i + 1, False, gate_part)
                gram(SG - 1, False)

            if stop >= 4:
                def wu_products(o, r):
                    if not (isinstance(o, int) and o < 1):
                        pe.wait_ge(sem("uw_taken"), o)
                    passed()
                    for c in range(8):
                        for q in hs:
                            last = mm(ps[0][q, 64 * c:64 * c + 64], TTs[r][q, c, :], VKAs[r][q, c, 0:64], start=True, stop=True)
                    last.then_inc(sem("wu_done"), 1)

                def mqbo(o, r, c):
                    if c == 0:
                        pe.wait_ge(sem("uw_taken"), o + 1)
                        if not (isinstance(o, int) and o < 1):
                            pe.wait_ge(sem("pt_ready"), o)
                            pe.wait_ge(sem("oi_ready"), o)
                            pe.wait_ge(sem("bt_ready"), o)
                            pe.wait_ge(sem("qt_ready"), o)
                        passed()
                    for q in hs:
                        mm(ps[1][q, 64 * c:64 * c + 64], UWs[r][q, c, CH:64], VKAs[r][q, c, CH:96], start=True, stop=True)
                    for q in hs:
                        last = mm(ps[2][q, 64 * c:64 * c + 64], UWs[r][q, c, 0:CH], VKAs[r][q, c, CH:96], start=True, stop=True)
                    if c == 7:
                        last.then_inc(sem("mqbo_done"), 1)

                def chain(o, r, k):
                    if k == 0:
                        pe.wait_ge(sem("pt_ready"), o + 1)
                    pe.wait_ge(sem("state_ready"), o * 4 + k + 1)
                    passed()
                    for b in range(B):
                        for q in hs:
                            last = mm(ps[3][q, CH * b:CH * b + CH], PTs[r][q, 4 * b + k, :], Sh[r][q, k, b, :], start=True, stop=True)
                    last.then_inc(sem("chain_done"), 1)

                def state_out(o, r):
                    pe.wait_ge(sem("qt_ready"), o + 1)
                    if not (isinstance(o, int) and o < 1):
                        pe.wait_ge(sem("delta_ready"), o)
                    passed()
                    for c in range(8):
                        for q in hs:
                            last = mm(ps[4][q, CH * c:CH * c + CH], Sh[r][q, c % 4, c // 4, :], QTs[r][q, c, :], start=True, stop=True)
                    last.then_inc(sem("state_out_done"), 1)

                def norms(o, r):
                    pe.wait_ge(sem("osq_ready"), o + 1)
                    if not (isinstance(o, int) and o < 1):
                        pe.wait_ge(sem("ors_ready"), o)
                    mm(ps[5][:, 0:256], bdm[:, :, :].rearrange("p h d -> p (h d)"), osq[r], start=True, stop=True).then_inc(sem("oss_done"), 1)

                def proj_out(o, r):
                    pe.wait_ge(sem("on_ready"), o + 1)
                    if not (isinstance(o, int) and o < 1):
                        pe.wait_ge(sem("attn_added"), o)
                    for b in range(B):
                        last = mm(ps[6][:, P * b:P * b + P], on[r][:, P * b:P * b + P], wo[:, :], start=True, stop=True)
                    last.then_inc(sem("wo_done"), 1)

                def iteration(i, r, octets_in=None):
                    for k in range(4):
                        if runs(i, 1):
                            chain(i - 1, 1 - r, k)
                        if runs(i, 0):
                            mqbo(i, r, 2 * k)
                            mqbo(i, r, 2 * k + 1)
                    if runs(i, -1):
                        pe.wait_ge(sem(f"octet_in_{1 - r}"), octets_in)
                        wu_products(i + 1, 1 - r)
                    if runs(i, 1):
                        state_out(i - 1, 1 - r)
                    if runs(i, 2):
                        norms(i - 2, r)
                    if runs(i, 4):
                        proj_out(i - 4, r)
                pe.wait_ge(sem("octet_in_0"), 32)
                wu_products(0, 0)
                for i in range(6):
                    iteration(i, i % 2, 32 * ((i + 1) // 2 + 1))
                with pe.Fori(3, NO // 2 - 1) as j:
                    iteration(j * 2, 0, j * 32 + 32)
                    iteration(j * 2 + 1, 1, j * 32 + 64)
                for i in range(NO - 2, NO + 4):
                    iteration(i, i % 2, 32 * ((i + 1) // 2 + 1))
            if stop >= 5:
                ffn(1)

        @block.scalar
        def _(act):
            a = nc.scalar.activation
            steps = Steps(act, sem("act_steps"))

            def take_weights():
                for n in range(NWT):
                    act.wait_ge(w_turned, n + 1)
                    if n < 3 * KT:
                        a(cw[:, n, :], ps[n % 4][:, 0:P], ACT.Copy).then_inc(w_taken, 1)
                    elif n < NWT - 1:
                        a(gw[:, n - 3 * KT, :], ps[n % 4][:, 0:P], ACT.Copy).then_inc(w_taken, 1)
                    else:
                        act.wait_ge(w_in, 16 * (6 + 3 * H + 1 + 2 * H))
                        a(wo[:, :], ps[n % 4][:, 0:P], ACT.Identity, scale=onw[:, 0:1]).then_inc(w_taken, 1)

            def root(n):
                act.wait_ge(sem(f"var_ready{n}"), 1)
                a(rstd[:, :], var[:, :], ACT.Sqrt, bias=ceps[:, 0:1]).then_inc(sem(f"std_ready{n}"), 1)

            def ffn(k):
                s = ffn_sems(k)
                act.wait_ge(consts, k + 1)
                root(k)

                def take(g, r):
                    act.wait_ge(s["xn_turned"], g + 1)
                    if not (isinstance(g, int) and g < 2):
                        act.wait_ge(s["logits_done"], g - 1)
                    a(YT[:, r].rearrange("p t d -> p (t d)"), ps[4 + 2 * r][:, :], ACT.Copy).then_inc(s["xnT_taken"], 1)
                take(0, 0)
                take(1, 1)
                with act.Fori(1, NG // 2) as j:
                    take(j * 2, 0)
                    take(j * 2 + 1, 1)
                act.wait_ge(s["z_ready"], 1)
                a(ex, ex, ACT.Exp).then_inc(s["exp_ready"], 1)
                if k == 0:
                    take_weights()

                def expert(j, r):
                    e = j * 2 + r
                    act.wait_ge(s["rows_used"], e + 1)
                    a(XET[:, r, :], ps[r][:, :], ACT.Copy).then_inc(s["rowsT_ready"], 1)
                    act.wait_ge(s["w1_used"], e + 1)
                    if not isinstance(j, int):
                        act.wait_ge(s["eout_done"], e - 1)
                    a(HT[:, r, :], ps[2 + r][:, :], ACT.Relu, bias=B1[:, ds(e, 1)]).then_inc(s["hidden_ready"], 1)
                expert(0, 0)
                expert(0, 1)
                with act.Fori(1, E // 2) as j:
                    for r in range(2):
                        expert(j, r)

            if stop >= 1:
                ffn(0)
            if stop >= 2:
                root("_a")

                for b in range(B):
                    with act.Fori(0, NG // B // 2) as j:
                        for r in range(2):
                            l = j * 2 + r
                            act.wait_ge(sem("xn_turned_a"), l + (NG // B) * b + 1)
                            a(XNT[:, b, ds(l * 512 + KT - 1, 512)], ps[4 + 2 * r][:, :], ACT.Copy).then_inc(sem("xnT_taken_a"), 1)

                def span(s, first):
                    for n in range(12):
                        kind, b = n // 2, n % 2
                        act.wait_ge(sem("proj_done"), s * 12 + n + 1)
                        if not first:
                            if n == 0:
                                act.wait_ge(sem("qk_chunked"), 2 * s - 1)
                            if n == 2:
                                act.wait_ge(sem("qk_chunked"), 2 * s)
                            if n == 4:
                                act.wait_ge(sem("v_chunked"), s)
                                act.wait_ge(sem("gv_ready"), s)
                            if n == 6:
                                act.wait_ge(sem("average_steps"), 2 * s)
                        src = ps[n % 4][:, :]
                        if kind < 3:
                            a((qT, kT, vT)[kind][:, b, :], src, ACT.Silu).then_inc(sem("silu_ready"), 1)
                            act.wait_ge(sem("silu_ready"), s * 6 + n + 1)
                        elif kind == 3:
                            a(ga[:, b, :], src, ACT.Sigmoid).then_inc(sem("gates_ready"), 1)
                            a(gb[:, b, :], src, ACT.Sigmoid, scale=-1.0).then_inc(sem("gates_ready"), 1)
                            act.wait_ge(sem("gates_ready"), s * 8 + 2 * b + 2)
                        elif kind == 4:
                            if not first and b == 0:
                                act.wait_ge(sem("beta_chunked"), s)
                            a(be[:, b, :], src, ACT.Sigmoid).then_inc(sem("gates_ready"), 1)
                            act.wait_ge(sem("gates_ready"), s * 8 + 5 + b)
                        else:
                            a(MX[:, b, ds(s * 512, 512)], src, ACT.Sigmoid, bias=mbias[:, 0:1]).then_inc(sem("gates_ready"), 1)
                            act.wait_ge(sem("gates_ready"), s * 8 + 7 + b)
                        act.sem_inc(sem("proj_free"), 1)
                    act.wait_ge(sem("qk_chunked"), 2 * s + 1)
                    a(sqq, qC, ACT.Square).then_inc(sem("sq_ready"), 1)
                    act.wait_ge(sem("qk_chunked"), 2 * s + 2)
                    if not first:
                        act.wait_ge(sem("gram_banks"), 4 * s)
                        act.wait_ge(sem("qn_kept"), s)
                    a(sqk, kC, ACT.Square).then_inc(sem("sq_ready"), 1)
                    act.wait_ge(sem("sums_ready"), 2 * s + 2)
                    a(rn[:, :, :], rn[:, :, :], ACT.Sqrt, bias=ceps[:, 2:3]).then_inc(sem("root_ready"), 1)
                span(0, True)
                with act.Fori(1, SG) as i:
                    span(i, False)

            if stop >= 4:
                def take_uw(o, r):
                    act.wait_ge(sem("wu_done"), o + 1)
                    a(UWs[r], chunks(ps[0][:, :], 64), ACT.Copy).then_inc(sem("uw_taken"), 1)

                def take_p_oi(o, r):
                    act.wait_ge(sem("mqbo_done"), o + 1)
                    a(PTs[r], chunks(ps[1][:, :], 64)[:, :, 0:CH], ACT.Copy).then_inc(sem("pt_ready"), 1)
                    if not (isinstance(o, int) and o < 2):
                        act.wait_ge(sem("delta_ready"), o - 1)
                    act.wait_ge(sem("bt_ready"), o + 1)
                    a(chunks(OIs[r]), chunks(ps[2][:, :], 64)[:, :, CH:64], ACT.Copy).then_inc(sem("oi_ready"), 1)

                def square(o, r):
                    act.wait_ge(sem("mixed_ready"), o + 1)
                    a(osq[r], om[r], ACT.Square).then_inc(sem("osq_ready"), 1)

                def rms(o, r):
                    act.wait_ge(sem("oss_done"), o + 1)
                    if not (isinstance(o, int) and o < 2):
                        act.wait_ge(sem("on_ready"), o - 1)
                    a(ors[r], ps[5][:, 0:256], ACT.Sqrt, bias=ceps[:, 1:2], scale=1.0 / CH).then_inc(sem("ors_ready"), 1)

                def iteration(i, r):
                    if runs(i, 2):
                        square(i - 2, r)
                    if runs(i, 0):
                        take_p_oi(i, r)
                    if runs(i, -1):
                        take_uw(i + 1, 1 - r)
                    if runs(i, 2):
                        rms(i - 2, r)
                take_uw(0, 0)
                for i in range(4):
                    iteration(i, i % 2)
                with act.Fori(2, NO // 2 - 1) as j:
                    iteration(j * 2, 0)
                    iteration(j * 2 + 1, 1)
                for i in range(NO - 2, NO + 2):
                    iteration(i, i % 2)
            if stop >= 5:
                ffn(1)

        @block.vector
        def _(dve):
            v = nc.vector
            st_ = Steps(dve, sem("dve_steps"))
            did = lambda i: st_.did(i)

            did(v.memset(XG[:, :, :], 0.0))
            st_.wait()
            dve.sem_inc(zero_ready, 1)
            def scale_weights():
                dve.wait_ge(w_in, 16 * (6 + 3 * H + 1 + 2 * H))
                for n in range(3 * KT):
                    v.tensor_scalar(wsc[n], wraw[:, n // KT, :], craw[:, n // KT, n % KT:n % KT + 1], None, ALU.mult).then_inc(w_scaled, 1)

            def all_means(n):
                for q in range(XQ):
                    if n == 0:
                        dve.wait_ge(sem(f"x_in_{q}"), 16)
                    with dve.Fori(q * NG // XQ, (q + 1) * NG // XQ) as g:
                        st_.enter(g, q * NG // XQ, TG)
                        for k in range(TG):
                            did(v.bn_stats(st[:, ds(g * TG + k, 1), :].rearrange("p t x -> p (t x)"),
                                           X[:, ds(g * TG + k, 1), :].rearrange("p t d -> p (t d)")))
                    st_.leave(NG // XQ)
                st_.wait()
                did(v.tensor_tensor(mean[:, :], st[:, :, 1], st[:, :, 4], ALU.subtract))
                did(v.tensor_tensor(var[:, :], st[:, :, 2], st[:, :, 5], ALU.add))
                st_.wait()
                did(v.scalar_tensor_tensor(out=rstd[:, :], in0=mean[:, :], scalar=0.25, in1=mean[:, :], op0=ALU.mult, op1=ALU.mult))
                st_.wait()
                did(v.tensor_tensor(mean[:, :], st[:, :, 1], st[:, :, 4], ALU.add))
                st_.wait()
                v.scalar_tensor_tensor(out=var[:, :], in0=var[:, :], scalar=1.0 / D, in1=rstd[:, :], op0=ALU.mult,
                                       op1=ALU.add).then_inc(sem(f"var_ready{n}"), 1)
                did(v.tensor_scalar(mean[:, :], mean[:, :], 0.5, None, ALU.mult))
                st_.wait()

            def invert(n):
                dve.wait_ge(sem(f"std_ready{n}"), 1)
                did(v.reciprocal(rstd[:, :], rstd[:, :]))
                st_.wait()

            def normalise(n):
                def body(g, r):
                    if not (isinstance(g, int) and g < 2):
                        dve.wait_ge(sem(f"xn_turned{n}"), g - 1)
                    for k in range(TG):
                        t1 = g * TG + k
                        v.tensor_scalar(XN[:, r, k, :], X[:, ds(t1, 1), :].rearrange("p t d -> p (t d)"), mean[:, ds(t1, 1)],
                                        rstd[:, ds(t1, 1)], ALU.subtract, ALU.mult).then_inc(sem(f"xn_ready{n}"), 1)
                body(0, 0)
                body(1, 1)
                with dve.Fori(1, NG // 2) as j:
                    body(j * 2, 0)
                    body(j * 2 + 1, 1)

            def ffn(k):
                s = ffn_sems(k)
                all_means(k)
                invert(k)
                normalise(k)
                dve.wait_ge(fw_in, 16 * 5 * (k + 1))
                dve.wait_ge(consts, k + 1)
                bce = lambda a: a.unsqueeze(2).to_broadcast([P, NT, E])
                bct = lambda a: a.unsqueeze(1).to_broadcast([P, NT, E])
                dve.wait_ge(s["logits_done"], NG)
                did(v.tensor_tensor(lg, ps[5][:, 0:NT * E].rearrange("p (t e) -> p t e", e=E), bct(brb), ALU.add))
                st_.wait()
                did(v.tensor_reduce(mx, lg, AX_X, ALU.max))
                st_.wait()
                v.tensor_tensor(ex, lg, bce(mx), ALU.subtract).then_inc(s["z_ready"], 1)
                did(v.tensor_tensor(eq, lg, bce(mx), ALU.is_equal))
                st_.wait()
                did(v.tensor_tensor(eq, eq, bct(rev), ALU.mult))
                st_.wait()
                did(v.tensor_reduce(mrev, eq, AX_X, ALU.max))
                st_.wait()
                v.tensor_tensor(oh, bct(rev), bce(mrev), ALU.is_equal).then_inc(s["onehot_ready"], 1)
                dve.wait_ge(s["exp_ready"], 1)
                did(v.tensor_reduce(sm, ex, AX_X, ALU.add))
                st_.wait()
                did(v.reciprocal(gate, sm))
                dve.wait_ge(s["ranks_done"], 1)
                did(v.tensor_copy(eview(tot), ps[7][:, 0:NT * E].rearrange("p (t e) -> p t e", e=E)))
                st_.wait()
                did(v.tensor_tensor_scan(incl, rmask, tot, 0.0, ALU.mult, ALU.add))
                st_.wait()
                did(v.tensor_tensor(incl, incl, tot, ALU.subtract))
                st_.wait()
                did(v.tensor_tensor(incl, incl, eoff, ALU.add))
                st_.wait()
                did(v.tensor_tensor(cum, ps[6][:, 0:NT * E].rearrange("p (t e) -> p t e", e=E), eview(incl), ALU.add))
                st_.wait()
                did(v.tensor_tensor(cum, cum, oh, ALU.mult))
                st_.wait()
                did(v.tensor_reduce(slot, cum, AX_X, ALU.add))
                st_.wait()
                did(v.scalar_tensor_tensor(out=tmp1, in0=mrev, scalar=float(CAP), in1=slot, op0=ALU.mult, op1=ALU.add))
                st_.wait()
                did(v.tensor_scalar(keep, tmp1, float(CAP * E + CAP), None, ALU.is_lt))
                st_.wait()
                did(v.tensor_tensor(gate, gate, keep, ALU.mult))
                did(v.tensor_tensor(gidx, slot, keep, ALU.mult))
                did(v.tensor_tensor(tmp1, slot, trash, ALU.subtract))
                st_.wait()
                did(v.tensor_tensor(tmp1, tmp1, keep, ALU.mult))
                did(v.tensor_scalar(hgate, gate, 0.5, None, ALU.mult))
                did(v.tensor_tensor(rstd[:, :], rstd[:, :], gate, ALU.mult))
                st_.wait()
                did(v.tensor_tensor(sidx, tmp1, trash, ALU.add))
                st_.wait()
                if k == 0:
                    dve.wait_ge(zeroed, 16 * E)
                with dve.Fori(0, NG) as g:
                    for j in range(TG):
                        t1 = g * TG + j
                        v.tensor_scalar(XG[:, ds(t1, 1), :].rearrange("p t d -> p (t d)"), X[:, ds(t1, 1), :].rearrange("p t d -> p (t d)"),
                                        mean[:, ds(t1, 1)], rstd[:, ds(t1, 1)], ALU.subtract, ALU.mult).then_inc(s["rows_ready"], 1)

                if k == 0:
                    scale_weights()

                def expert(j, r):
                    e = j * 2 + r
                    dve.wait_ge(s["eout_done"], e + 1)
                    if not isinstance(j, int):
                        dve.wait_ge(s["stored"][r], j * 16)
                    v.tensor_tensor(EO[:, r], ps[4 + r][:, :].rearrange("p (s d) -> p s d", s=4),
                                    B2[:, ds(e, 1), :].to_broadcast([P, 4, D]), ALU.add).then_inc(s["eout_ready"], 1)
                expert(0, 0)
                expert(0, 1)
                with dve.Fori(1, E // 2) as j:
                    for r in range(2):
                        expert(j, r)
                for g in range(NG):
                    dve.wait_ge(sem(f"gathered{k}_{g}"), 16 * TG)
                    for j in range(TG):
                        n = g * TG + j
                        v.scalar_tensor_tensor(out=X[:, n, :], in0=XG[:, n, :], scalar=hgate[:, n:n + 1], in1=X[:, n, :],
                                               op0=ALU.mult, op1=ALU.add).then_inc(sem(f"added{k}"), 1)
                dve.wait_ge(sem(f"added{k}"), NT)

            if stop >= 1:
                ffn(0)

            if stop >= 2:
                all_means("_a")
                invert("_a")
                normalise("_a")

                turned = lambda a: a.rearrange("p b (q x) -> p q b x", x=P)
                row = lambda a: a.rearrange("p m d -> p (m d)")

                def front(s, first):
                    if not first:
                        dve.wait_ge(sem("qn_kept"), s)
                    dve.wait_ge(sem("silu_ready"), 6 * s + 2)
                    v.transpose(row(qC), turned(qT)).then_inc(sem("qk_chunked"), 1)
                    dve.wait_ge(sem("silu_ready"), 6 * s + 4)
                    v.transpose(row(kC), turned(kT)).then_inc(sem("qk_chunked"), 1)
                    dve.wait_ge(sem("silu_ready"), 6 * s + 6)
                    v.transpose(row(vC), turned(vT)).then_inc(sem("v_chunked"), 1)
                    dve.wait_ge(sem("gates_ready"), 8 * s + 6)
                    v.transpose(row(bC), turned(be)).then_inc(sem("beta_chunked"), 1)
                    dve.wait_ge(sem("sq_ready"), 2 * s + 1)
                    v.tensor_reduce(rn[:, 0, :], sqq, AX_X, ALU.add).then_inc(sem("sums_ready"), 1)
                    dve.wait_ge(sem("sq_ready"), 2 * s + 2)
                    v.tensor_reduce(rn[:, 1, :], sqk, AX_X, ALU.add).then_inc(sem("sums_ready"), 1)
                    dve.wait_ge(sem("beta_chunked"), s + 1)
                    did(v.tensor_scalar(nbeta[:, ds(s * M, M)], bC[:, :, 0], -1.0, None, ALU.mult))
                    did(v.tensor_copy(beta[:, ds(s * M, M)], bC[:, :, 0]))
                    dve.wait_ge(sem("gv_ready"), s + 1)
                    if not first:
                        dve.wait_ge(sem("average_steps"), 2 * s)
                    for b in range(B):
                        v.tensor_tensor_scan(EM[:, b, ds(s * 512, 512)], ga[:, b, :], gb[:, b, :],
                                             0.0 if first else EM[:, b, ds(s * 512 - 1, 1)], ALU.mult, ALU.add).then_inc(sem("average_steps"), 1)
                    dve.wait_ge(sem("root_ready"), s + 1)
                    did(v.reciprocal(rn[:, :, :], rn[:, :, :]))
                    st_.wait()
                    did(v.tensor_tensor(qC, qC, rn[:, 0, :].unsqueeze(2).to_broadcast([P, M, CH]), ALU.mult))
                    v.tensor_tensor(kC, kC, rn[:, 1, :].unsqueeze(2).to_broadcast([P, M, CH]), ALU.mult).then_inc(sem("k_normed"), 1)
                    st_.wait()
                    v.transpose(KQ[:, :, CH:64], qC).then_inc(sem("kq_ready"), 1)
                    dve.wait_ge(sem("k_normed"), s + 1)
                    v.transpose(KQ[:, :, 0:CH], kC).then_inc(sem("kq_ready"), 1)

                def solve(s, fronts):
                    dve.wait_ge(sem("kq_ready"), 2 * fronts)
                    for n in range(M // 8):
                        dve.wait_ge(sem("gram_banks"), 4 * s + n + 1)
                        pv = ps[4 + n][:, :].rearrange("p (c x) -> p c x", x=64)
                        v.tensor_tensor(AG[:, 8 * n:8 * n + 8, :], pv[:, :, 0:CH],
                                        nbeta[:, ds(s * M + 8 * n, 8)].unsqueeze(2).to_broadcast([P, 8, CH]), ALU.mult).then_inc(sem("gram_taken"), 1)
                        v.tensor_tensor(VKA[:, ds(s * M + 8 * n, 8), 64:96], pv[:, :, CH:64],
                                        triu[:, :].unsqueeze(1).to_broadcast([P, 8, CH]), ALU.mult).then_inc(sem("gram_taken"), 1)
                    did(v.memset(row(RT), 0.0))
                    dve.wait_ge(sem("gram_taken"), 8 * s + 8)
                    did(v.transpose(RA, AG.rearrange("p m j -> p j m")))
                    st_.wait(1)
                    did(v.memset(row(RT)[:, 0:CH * CH:CH + 1], 1.0))
                    st_.wait()
                    for j in range(CH - 1):
                        n = CH - 1 - j
                        cuts = [(j + 1, CH)] if n < 3 else [(j + 1, j + 1 + (n + 1) // 2), (j + 1 + (n + 1) // 2, CH)]
                        back = len(cuts) - 1
                        w = j + 1
                        parts = []
                        for lo, hi in cuts:
                            pr = prod[j % 2][:, (lo - j - 1) * w:(hi - j - 1) * w].rearrange("p (i c) -> p i c", c=w)
                            did(v.tensor_tensor(pr, RA[:, j, lo:hi].unsqueeze(2).to_broadcast([P, hi - lo, w]),
                                                RT[:, j:j + 1, 0:w].to_broadcast([P, hi - lo, w]), ALU.mult))
                            parts.append((lo, hi, pr))
                        for lo, hi, pr in parts:
                            st_.wait(back)
                            did(v.tensor_tensor(RT[:, lo:hi, 0:w], RT[:, lo:hi, 0:w], pr, ALU.add))
                        st_.wait(back)
                    st_.wait()
                    did(v.transpose(TC.rearrange("p m i -> p i m"), RT))
                    st_.wait()
                    v.tensor_tensor(TT[:, ds(s * 1024, 1024)].rearrange("p (m d) -> p m d", d=CH), TC,
                                    beta[:, ds(s * M, M)].unsqueeze(2).to_broadcast([P, M, CH]), ALU.mult).then_inc(sem("tt_ready"), 1)
                    dve.wait_ge(sem("tt_ready"), s + 1)

                split = sum(2 if CH - 1 - j < 3 else 4 for j in range(CH - 1))
                front(0, True)
                with dve.Fori(0, SG - 1) as i:
                    st_.enter(i, 0, 4 + 3 + split + 1)
                    front(i + 1, False)
                    solve(i, i + 2)
                st_.leave(SG - 1)
                dve.wait_ge(sem("qn_kept"), SG)
                solve(SG - 1, SG)

            if stop >= 4:
                v.memset(Sh[0][:, 0], 0.0).then_inc(sem("state_ready"), 1)

                def state_plus_b(o, r, k):
                    dve.wait_ge(sem("state_ready"), o * 4 + k + 1)
                    if k == 0:
                        dve.wait_ge(sem("bt_ready"), o + 1)
                    v.tensor_tensor(both(SBs), Sh[r][:, k], BTs[r][:, k:8:4, :], ALU.add).then_inc(sem("sb_ready"), 1)

                def next_state(o, r, k):
                    dve.wait_ge(sem("sb_ready"), o * 4 + k + 1)
                    dve.wait_ge(sem("chain_done"), o * 4 + k + 1)
                    dst = Sh[r][:, k + 1] if k < 3 else Sh[1 - r][:, 0]
                    v.tensor_tensor(dst, both(SBs), both(ps[3][:, 0:B * CH]), ALU.subtract).then_inc(sem("state_ready"), 1)

                def take_b_q(o, r):
                    dve.wait_ge(sem("mqbo_done"), o + 1)
                    v.transpose(BTs[r], chunks(ps[2][:, :], 64)[:, :, 0:CH]).then_inc(sem("bt_ready"), 1)
                    dve.wait_ge(sem("pt_ready"), o + 1)
                    v.tensor_tensor(QTs[r], QN[:, ds(o * 8, 8), :], chunks(ps[1][:, :], 64)[:, :, CH:64],
                                    ALU.subtract).then_inc(sem("qt_ready"), 1)

                def delta(o, r):
                    dve.wait_ge(sem("state_out_done"), o + 1)
                    dve.wait_ge(sem("oi_ready"), o + 1)
                    if not (isinstance(o, int) and o < 2):
                        dve.wait_ge(sem("gated_ready"), o - 1)
                        dve.wait_ge(sem("mixed_ready"), o - 1)
                    v.tensor_tensor(od[r], ps[4][:, 0:256], OIs[r], ALU.add).then_inc(sem("delta_ready"), 1)

                def mixed(o, r):
                    dve.wait_ge(sem("gated_ready"), o + 1)
                    dve.wait_ge(sem("delta_ready"), o + 1)
                    if not (isinstance(o, int) and o < 2):
                        dve.wait_ge(sem("osq_ready"), o - 1)
                        dve.wait_ge(sem("on_ready"), o - 1)
                    v.tensor_tensor(om[r], od[r], dm[r], ALU.add).then_inc(sem("mixed_ready"), 1)

                def scaled(o, r):
                    dve.wait_ge(sem("ors_ready"), o + 1)
                    v.reciprocal(ors[r], ors[r]).then_inc(sem("inverse_ready"), 1)
                    dve.wait_ge(sem("inverse_ready"), o + 1)
                    if not (isinstance(o, int) and o < 2):
                        dve.wait_ge(sem("wo_done"), o - 1)
                    v.tensor_tensor(on[r], om[r], ors[r], ALU.mult).then_inc(sem("on_ready"), 1)

                def residual(o):
                    dve.wait_ge(sem("wo_done"), o + 1)
                    xo = X[:, :, :].rearrange("p (b t) d -> p b t d", b=B)[:, :, ds(o, 1), :].rearrange("p b t d -> p b (t d)")
                    v.tensor_tensor(xo, xo, both(ps[6][:, 0:256]), ALU.add).then_inc(sem("attn_added"), 1)

                def iteration(i, r):
                    for k in range(4):
                        if runs(i, 1):
                            if k > 0:
                                state_plus_b(i - 1, 1 - r, k)
                            next_state(i - 1, 1 - r, k)
                        if k == 0 and runs(i, 2):
                            delta(i - 2, r)
                        if k == 2 and runs(i, 5):
                            residual(i - 5)
                        if k == 3 and runs(i, 2):
                            mixed(i - 2, r)
                    if runs(i, 0):
                        take_b_q(i, r)
                        state_plus_b(i, r, 0)
                    if runs(i, 3):
                        scaled(i - 3, 1 - r)
                for i in range(6):
                    iteration(i, i % 2)
                with dve.Fori(3, NO // 2) as j:
                    iteration(j * 2, 0)
                    iteration(j * 2 + 1, 1)
                for i in range(NO, NO + 5):
                    iteration(i, i % 2)
                dve.wait_ge(sem("attn_added"), NO)
                dve.sem_inc(sem("attn_done"), 1)
            if stop >= 5:
                ffn(1)
            if dump is not None:
                dve.drain().then_inc(sem("fin"), 1)


_INS = ["L0_attn_hidden_states", "L0_attn_Wq", "L0_attn_Wk", "L0_attn_Wv", "L0_attn_Wb", "L0_attn_Wdec",
        "L0_attn_Wmix", "L0_attn_mix_bias", "L0_attn_wq_conv", "L0_attn_wk_conv", "L0_attn_wv_conv",
        "L0_attn_onorm_w", "L0_attn_Wo", "L0_ffn_Wr", "L0_ffn_br", "L0_ffn_W1", "L0_ffn_b1", "L0_ffn_W2",
        "L0_ffn_b2"]


def kernel(**inputs):
    import numpy as _np
    import concourse.bacc as _bacc
    from concourse import mybir as _mybir
    from concourse.bass_utils import run_bass_kernel_spmd as _run

    nc = _bacc.Bacc("TRN2", target_bir_lowering=False, num_devices=1)
    arrays, tensors = {}, {}
    for name in _INS:
        a = _np.ascontiguousarray(inputs[name])
        arrays[f"in_{name}"] = a
        tensors[name] = nc.dram_tensor(f"in_{name}", a.shape, _mybir.dt.from_np(a.dtype), kind="ExternalInput").ap()
    shape = tuple(inputs["L0_attn_hidden_states"].shape)
    out = nc.dram_tensor("out_x", shape, _mybir.dt.from_np(_np.dtype("float32")), kind="ExternalOutput").ap()
    macaron_kernel(nc, tensors, out)
    r = _run(nc, [arrays], core_ids=[0])
    return r.results[0]["out_x"]
```

```python
import concourse.bass as bass
from concourse import mybir
from contextlib import ExitStack

F32 = mybir.dt.float32
BF16 = mybir.dt.bfloat16
U32 = mybir.dt.uint32
ALU = mybir.AluOpType
ACT = mybir.ActivationFunctionType
AX_X = mybir.AxisListType.X
ds = bass.ds

P = 128
CH = 32
EPS_LN = 1e-5
EPS_L2 = 1e-6
EPS_RMS = 1e-5


class Steps:

    def __init__(self, eng, sem):
        self.eng, self.sem = eng, sem
        self.base, self.local, self.reg, self.first, self.per = 0, 0, None, 0, 0

    def did(self, instruction):
        instruction.then_inc(self.sem, 1)
        self.local += 1
        return instruction

    def value(self, back=0):
        v = self.base + self.local - back
        return v if self.reg is None else (self.reg - self.first) * self.per + v

    def wait(self, back=0):
        self.eng.wait_ge(self.sem, self.value(back))

    def enter(self, reg, first, per):
        self.base += self.local
        self.reg, self.first, self.per, self.local = reg, first, per, 0

    def leave(self, times):
        assert self.local == self.per, (self.local, self.per)
        self.base += self.per * times
        self.reg, self.local = None, 0


class Fields:

    def __init__(self, W2, B2, B1, wr, brb, rmask, eoff, trash, rev, iota, tri, onesb):
        self.W2, self.B2, self.B1, self.wr, self.brb = W2, B2, B1, wr, brb
        self.rmask, self.eoff, self.trash, self.rev = rmask, eoff, trash, rev
        self.iota, self.tri, self.onesb = iota, tri, onesb


def macaron_kernel(nc, t, out):
    x_d = t["L0_attn_hidden_states"]
    B, L, D = x_d.shape
    H = t["L0_attn_Wb"].shape[0]
    KT = t["L0_attn_wq_conv"].shape[1]
    E = t["L0_ffn_Wr"].shape[1]
    N = B * L
    CAP = N // E
    NT = N // P
    TG = 4
    NG = NT // TG
    SG = L // 512
    NO = L // P
    M = 2 * 512 // CH
    assert (B, D, H * CH, CAP, M) == (2, P, P, 512, 32)

    x_v = x_d.rearrange("b (t p) d -> p (b t) d", p=P)
    out_v = out.rearrange("b (t p) d -> p (b t) d", p=P)
    slots_d = nc.dram_tensor("expert_rows", [2 * N, D], F32).ap()
    eout_d = nc.dram_tensor("expert_out", [N, D], F32).ap()
    slots_v = slots_d[0:N, :].rearrange("(e p s) d -> e p (s d)", p=P, s=CAP // P)
    eout_v = eout_d.rearrange("(e p s) d -> e p (s d)", p=P, s=CAP // P)

    ctx = ExitStack()
    with ctx:
        def sb(name, shape, dt=F32):
            return ctx.enter_context(nc.sbuf_tensor(name, shape, dt))

        sems = {}

        def sem(name):
            if name not in sems:
                sems[name] = ctx.enter_context(nc.semaphore(name))
            return sems[name]

        ps = [ctx.enter_context(nc.psum_tensor(f"bank{i}", [P, 512], F32)) for i in range(8)]

        X = sb("X", [P, NT, D])
        XG = sb("XG", [P, NT, D])
        XNT = sb("XNT", [P, B, L + KT - 1])
        VKA = sb("VKA", [P, NO * 8, 96])
        QN = sb("QN", [P, NO * 8, CH])
        EM = sb("EM", [P, B, L])
        MX = sb("MX", [P, B, L])
        W = [sb(f"W{i}", [P, 1024]) for i in range(11)]
        KQ = sb("KQ", [P, M, 64])
        TT = XG[:, :, :].rearrange("p t d -> p (t d)")

        ident = sb("ident", [P, P])
        bdm = sb("bdm", [P, H, CH])
        triu = sb("triu", [P, CH])
        cw = sb("cw", [P, 3 * KT, P])
        gw = sb("gw", [P, 3, P])
        wo = sb("wo", [P, P])
        mbias = sb("mbias", [P, 1])
        onw = sb("onw", [P, 1])
        ones = sb("ones", [P, B])
        ceps = sb("ceps", [P, 3])
        mean = sb("mean", [P, NT])
        mv = sb("mv", [P, NT, 2])
        var = sb("var", [P, NT])
        rstd = sb("rstd", [P, NT])
        rn = sb("rn", [P, 2, M])
        beta = sb("beta", [P, NO * 8])
        nbeta = sb("nbeta", [P, NO * 8])

        def carve(space):
            used = [0]

            def piece(n):
                used[0] += n
                assert used[0] <= space.shape[1]
                return space[:, used[0] - n:used[0]]
            return piece
        part = carve(VKA[:, :, :].rearrange("p m c -> p (m c)"))

        XE = part(2 * 512).rearrange("p (r s d) -> p r s d", r=2, s=4)
        EO = part(2 * 512).rearrange("p (r s d) -> p r s d", r=2, s=4)
        HT = part(2 * 512).rearrange("p (r n) -> p r n", r=2)
        XET = part(2 * 512).rearrange("p (r n) -> p r n", r=2)
        W1 = part(2 * 128).rearrange("p (r n) -> p r n", r=2)
        XN = part(2 * TG * D).rearrange("p (r t d) -> p r t d", r=2, t=TG)
        YT = part(2 * TG * D).rearrange("p (r t d) -> p r t d", r=2, t=TG)
        te = lambda: part(NT * E).rearrange("p (t e) -> p t e", e=E)
        lg, eq, ex, cum = te(), te(), te(), te()
        tot, incl = part(NT * E), part(NT * E)
        mx, sm, gate, keep, hgate, slot, tmp1, mrev = [part(NT) for _ in range(8)]
        sidx = part(NT).bitcast(U32)
        gidx = part(NT).bitcast(U32)
        oh = part(NT * E // 2).bitcast(BF16).rearrange("p (t e) -> p t e", e=E)

        def constants(part):
            return Fields(
                W2=part(E * D).rearrange("p (e n) -> p e n", e=E), B2=part(E * D).rearrange("p (e n) -> p e n", e=E),
                B1=part(E), wr=part(E), brb=part(E),
                rmask=part(NT * E),
                eoff=part(NT * E),
                trash=part(NT),
                rev=part(E),
                iota=part(NT * E).bitcast(mybir.dt.int32),
                tri=part(P // 2).bitcast(BF16),
                onesb=part(P // 2).bitcast(BF16))
        fc = [constants(part), constants(carve(XNT[:, :, :].rearrange("p b l -> p (b l)")))]

        HN = NT // 2
        half = lambda a, h: a[:, h * HN * E:(h + 1) * HN * E]
        by_tile = lambda a: a.rearrange("p (t e) -> p t e", e=E)
        by_expert = lambda a: a.rearrange("p (e t) -> p e t", e=E)
        eview = lambda a: a.rearrange("p (e t) -> p t e", e=E)

        st = W[9][:, 512:512 + NT * 6].rearrange("p (t x) -> p t x", x=6)
        turns = [b * NG // B + l for l in range(NG // B) for b in range(B)]

        def bt(i):
            return W[i][:, :].rearrange("p (b l) -> p b l", b=B)
        qT, kT, vT, ga, gb, be = [bt(i) for i in range(6)]
        qC, kC, vC, bC = [W[i][:, :].rearrange("p (m d) -> p m d", d=CH) for i in (6, 7, 8, 9)]
        sqq, sqk = [W[i][:, :].rearrange("p (m d) -> p m d", d=CH) for i in (0, 1)]
        AG = qC
        TC = qC
        RA = W[10][:, :].rearrange("p (j i) -> p j i", j=CH)
        RT = W[9][:, :].rearrange("p (i c) -> p i c", c=CH)
        prod = [W[6][:, 0:512], W[6][:, 512:1024]]

        chunks = lambda a, n=CH: a.rearrange("p (c d) -> p c d", d=n)
        heads = lambda w: w[:, :].rearrange("p (c h d) -> p c h d", c=8, h=H)
        quarters = [W[w][:, 256 * k:256 * k + 256] for w in range(5, 10) for k in range(4)]
        ring = lambda n: [quarters[2 * n], quarters[2 * n + 1]]
        BDT = heads(W[0])
        BDU = [heads(W[1]), heads(W[2])]
        BDW = [heads(W[3]), heads(W[4])]
        PQs = [chunks(W[10][:, 0:512], 64), chunks(W[10][:, 512:1024], 64)]
        BDS = [a.rearrange("p (b h d) -> p b h d", b=B, h=H) for a in ring(0)]
        eg = ring(1)
        mi = ring(2)
        od = ring(3)
        om = ring(4)
        osq = ring(5)
        ors = ring(6)
        on = ring(7)
        Sc = quarters[16][:, 0:B * CH]
        dT = quarters[17][:, 0:B * CH]
        both = lambda a: a.rearrange("p (b x) -> p b x", b=B)

        def ffn_sems(k):
            return {n: sem(f"{n}{k}") for n in (
                "xn_ready", "xn_turned", "xnT_taken",
                "logits_done", "z_ready", "exp_ready", "onehot_ready", "ranks_done", "rows_ready",
                "scattered", "w1_used", "rows_used", "rowsT_ready",
                "hidden_ready", "eout_done", "eout_ready", "added")} | {
                n: [sem(f"{n}{k}_{r}") for r in range(2)] for n in ("w1_in", "rows_in", "stored")}

        XQ = 4
        w_in = sem("w_in")
        fw_in = sem("fw_in")
        zero_ready = sem("zero_ready")
        zeroed = sem("zeroed")
        consts = sem("consts")
        w_scaled = sem("w_scaled")
        w_turned = sem("w_turned")
        w_taken = sem("w_taken")
        NWT = 3 * KT + 4
        NP = 12

        block = ctx.enter_context(nc.Block())

        wsrc = [(t["L0_attn_Wq"], t["L0_attn_wq_conv"]), (t["L0_attn_Wk"], t["L0_attn_wk_conv"]),
                (t["L0_attn_Wv"], t["L0_attn_wv_conv"])]
        wraw = W[0][:, 0:3 * P].rearrange("p (n d) -> p n d", n=3)
        graw = W[0][:, 3 * P:6 * P].rearrange("p (n d) -> p n d", n=3)
        woraw = W[0][:, 6 * P:7 * P]
        craw = W[0][:, 7 * P:7 * P + 3 * KT].rearrange("p (n j) -> p n j", n=3)
        wsc = [W[1 + n // 8][:, P * (n % 8):P * (n % 8) + P] for n in range(3 * KT)]

        def runs(i, lag):
            return not isinstance(i, int) or 0 <= i - lag < NO

        @block.sync
        def _(sp):
            def load_ffn(k):
                f = fc[k]
                sp.dma_start(f.wr, t["L0_ffn_Wr"]).then_inc(fw_in, 16)
                sp.dma_start(f.brb, t["L0_ffn_br"].rearrange("(a e) -> a e", a=1).broadcast_to([P, E])).then_inc(fw_in, 16)
                sp.dma_start(f.B1, t["L0_ffn_b1"].rearrange("e f -> f e")).then_inc(fw_in, 16)
                sp.dma_start(f.B2, t["L0_ffn_b2"].rearrange("(a e) d -> a e d", a=1).broadcast_to([P, E, D])).then_inc(fw_in, 16)
                sp.dma_start(f.W2, t["L0_ffn_W2"].rearrange("e f d -> f e d")).then_inc(fw_in, 16)

            for n in range(XQ):
                q = slice(n * NT // XQ, (n + 1) * NT // XQ)
                sp.dma_start(X[:, q, :], x_v[:, q, :]).then_inc(sem(f"x_in_{n}"), 16)
            with nc.allow_non_contiguous_dma(reason="small"):
                load_ffn(0)
            sp.wait_ge(zero_ready, 1)
            for e in range(E):
                sp.dma_start(slots_v[e], XG[:, 4 * e:4 * e + 4, :].rearrange("p s d -> p (s d)")).then_inc(zeroed, 16)
            with nc.allow_non_contiguous_dma(reason="small"):
                for n, (w, c) in enumerate(wsrc):
                    sp.dma_start(wraw[:, n, :], w).then_inc(w_in, 16)
                    sp.dma_start(craw[:, n, :], c).then_inc(w_in, 16)
                for n, w in enumerate(("L0_attn_Wdec", "L0_attn_Wb", "L0_attn_Wmix")):
                    for h in range(H):
                        sp.dma_start(graw[CH * h:CH * h + CH, n, :], t[w][h:h + 1, :].broadcast_to([CH, D])).then_inc(w_in, 16)
                sp.dma_start(woraw, t["L0_attn_Wo"]).then_inc(w_in, 16)
                for h in range(H):
                    sp.dma_start(mbias[CH * h:CH * h + CH, :], t["L0_attn_mix_bias"].rearrange(
                        "(h a) -> h a", a=1)[h:h + 1, :].broadcast_to([CH, 1])).then_inc(w_in, 16)
                    sp.dma_start(onw[CH * h:CH * h + CH, :], t["L0_attn_onorm_w"].rearrange("(d a) -> d a", a=1)).then_inc(w_in, 16)

            def ffn_io(k):
                s = ffn_sems(k)

                def load_w1(j, r):
                    if not isinstance(j, int):
                        sp.wait_ge(s["w1_used"], j * 2 + r - 1)
                    sp.dma_start(W1[:, r, :], t["L0_ffn_W1"][ds(j * 2 + r, 1)].rearrange("e d f -> (e d) f")).then_inc(s["w1_in"][r], 16)

                def load_rows(j, r):
                    if not isinstance(j, int):
                        sp.wait_ge(s["rows_used"], j * 2 + r - 1)
                    sp.dma_start(XE[:, r].rearrange("p s d -> p (s d)"),
                                 slots_v[ds(j * 2 + r, 1)].rearrange("e p x -> (e p) x")).then_inc(s["rows_in"][r], 16)

                def store(j, r):
                    e = j * 2 + r
                    sp.wait_ge(s["eout_ready"], e + 1)
                    sp.dma_start(eout_v[ds(e, 1)].rearrange("e p x -> (e p) x"),
                                 EO[:, r].rearrange("p s d -> p (s d)")).then_inc(s["stored"][r], 16)
                if k:
                    sp.wait_ge(sem("proj_done"), NP * SG)
                    with nc.allow_non_contiguous_dma(reason="small"):
                        load_ffn(1)
                    sp.wait_ge(sem("attn_done"), 1)
                load_w1(0, 0)
                load_w1(0, 1)
                sp.wait_ge(s["scattered"], 16 * NT)
                load_rows(0, 0)
                load_rows(0, 1)
                with sp.Fori(0, E // 2 - 1) as j:
                    for r in range(2):
                        load_rows(j + 1, r)
                        load_w1(j + 1, r)
                        store(j, r)
                store(E // 2 - 1, 0)
                store(E // 2 - 1, 1)

            ffn_io(0)
            ffn_io(1)
            with sp.Fori(0, NG) as g:
                sp.wait_ge(sem("added1"), g * TG + TG)
                sp.dma_start(out_v[:, ds(g * TG, TG), :], X[:, ds(g * TG, TG), :]).then_inc(sem("out_in"), 16)
            sp.wait_ge(sem("out_in"), 16 * NG)

        @block.gpsimd
        def _(pool):
            g = nc.gpsimd
            pool_steps = Steps(pool, sem("pool_steps"))

            def one(instruction):
                pool_steps.did(instruction)
                pool_steps.wait()

            def make_consts():
                one(g.memset(ident[:, :], 0.0))
                one(g.memset(bdm[:, :, :], 0.0))
                one(g.memset(triu[:, :], 1.0))
                one(g.memset(ceps[:, 0:1], EPS_LN))
                one(g.memset(ceps[:, 1:2], EPS_RMS))
                one(g.memset(ceps[:, 2:3], EPS_L2))
                one(g.memset(ones[:, :], 1.0))
                one(g.memset(XNT[:, :, 0:KT - 1], 0.0))
                one(g.affine_select(out=ident[:, :], in_=ident[:, :], compare_op=ALU.not_equal, fill=1.0,
                                base=0, pattern=[[-1, P]], channel_multiplier=1))
                for h in range(H):
                    q = slice(CH * h, CH * h + CH)
                    one(g.memset(bdm[q, h, :], 1.0))
                    one(g.affine_select(out=triu[q, :], in_=triu[q, :], compare_op=ALU.is_ge, fill=0.0,
                                    base=0, pattern=[[1, CH]], channel_multiplier=-1))

            def ffn_consts(k):
                f = fc[k]
                one(g.memset(f.onesb, 1.0))
                one(g.memset(f.tri, 1.0))
                one(g.memset(f.rmask, 1.0))
                one(g.affine_select(out=f.tri, in_=f.tri, compare_op=ALU.is_ge, fill=0.0, base=0,
                                pattern=[[1, P]], channel_multiplier=-1))
                one(g.memset(f.rmask.rearrange("p (e t) -> p e t", t=HN)[:, :, 0:1], 0.0))
                one(g.iota(f.iota[:, 0:E], pattern=[[-1, E]], base=E, channel_multiplier=0))
                one(g.tensor_copy(f.rev, f.iota[:, 0:E]))
                one(g.iota(f.iota[:, 0:NT], pattern=[[P, NT]], base=N, channel_multiplier=1))
                one(g.tensor_copy(f.trash, f.iota[:, 0:NT]))
                one(g.iota(f.iota, pattern=[[0, 2], [CAP, E], [0, HN]], base=0, channel_multiplier=0))
                g.tensor_copy(f.eoff, f.iota).then_inc(consts, 1)

            make_consts()
            ffn_consts(0)

            def ffn_moves(k):
                s = ffn_sems(k)
                if k == 0:
                    pool.wait_ge(zeroed, 16 * E)
                for n in range(NT):
                    pool.wait_ge(s["rows_ready"], n + 1)
                    g.indirect_dma_start(slots_d, bass.IndirectOffsetOnAxis(ap=sidx[:, n:n + 1], axis=0),
                                         XG[:, n, :], None).then_inc(s["scattered"], 16)
                for r in range(2):
                    pool.wait_ge(s["stored"][r], 16 * (E // 2))
                for grp in (turns if k == 0 else range(NG)):
                    for n in range(grp * TG, grp * TG + TG):
                        g.indirect_dma_start(XG[:, n, :], None, eout_d,
                                             bass.IndirectOffsetOnAxis(ap=gidx[:, n:n + 1], axis=0)).then_inc(
                                                 sem(f"gathered{k}_{grp}"), 16)

            ffn_moves(0)

            flat_rt = RT.rearrange("p i c -> p (i c)")

            def span(s, first):
                pool.wait_ge(sem("silu_ready"), 6 * s + 6)
                pool.wait_ge(sem("gates_ready"), 8 * s + 4)
                g.tensor_tensor(gb, gb, vT, ALU.mult).then_inc(sem("gv_ready"), 1)
                pool.wait_ge(sem("v_chunked"), s + 1)
                g.tensor_copy(VKA[:, ds(s * M, M), 0:CH], vC)
                pool.wait_ge(sem("norms_ready"), s + 1)
                g.tensor_tensor(kC, kC, rn[:, 1, :].unsqueeze(2).to_broadcast([P, M, CH]), ALU.mult).then_inc(sem("k_normed"), 1)
                if not first:
                    g.memset(flat_rt, 0.0).then_inc(sem("rt_cleared"), 1)
                    pool.wait_ge(sem("rt_cleared"), s)
                pool.wait_ge(sem("k_normed"), s + 1)
                g.tensor_copy(VKA[:, ds(s * M, M), CH:64], kC)
                if not first:
                    g.memset(flat_rt[:, 0:CH * CH:CH + 1], 1.0).then_inc(sem("rt_ready"), 1)
                pool.wait_ge(sem("kq_ready"), 2 * s + 2)
                g.tensor_copy(QN[:, ds(s * M, M), :], KQ[:, :, CH:64]).then_inc(sem("qn_kept"), 1)
                if not first:
                    mask(s - 1)

            def mask(s):
                pool.wait_ge(sem("a_copied"), 4 * s + 4)
                a = VKA[:, ds(s * M, M), 64:96]
                g.tensor_tensor(a, a, triu[:, :].unsqueeze(1).to_broadcast([P, M, CH]), ALU.mult).then_inc(sem("a_masked"), 1)

            span(0, True)
            with pool.Fori(1, SG) as i:
                span(i, False)
            mask(SG - 1)
            pool.wait_ge(sem("proj_done"), NP * SG)
            ffn_consts(1)
            pool.wait_ge(sem("tt_ready"), SG - 1)
            g.memset(flat_rt, 0.0).then_inc(sem("rt_cleared"), 1)
            pool.wait_ge(sem("rt_cleared"), SG)
            g.memset(flat_rt[:, 0:CH * CH:CH + 1], 1.0).then_inc(sem("rt_ready"), 1)

            def blocks(o):
                if not (isinstance(o, int) and o < 1):
                    pool.wait_ge(sem("wu_done"), o)
                g.tensor_tensor(BDT, TT[:, ds(o * 256, 256)].rearrange("p (c d) -> p c d", d=CH).unsqueeze(2).to_broadcast([P, 8, H, CH]),
                                bdm[:, :, :].unsqueeze(1).to_broadcast([P, 8, H, CH]), ALU.mult).then_inc(sem("bdt_ready"), 1)

            def gates(o, r):
                if not (isinstance(o, int) and o < 2):
                    pool.wait_ge(sem("mixed_ready"), o - 1)
                mix = MX[:, :, ds(o * P, P)]
                g.tensor_tensor(both(mi[r]), ones[:, :].unsqueeze(2).to_broadcast([P, B, P]), mix,
                                ALU.subtract).then_inc(sem("mixing_ready"), 1)
                g.tensor_tensor(both(eg[r]), EM[:, :, ds(o * P, P)], mix, ALU.mult).then_inc(sem("mixing_ready"), 1)

            def mixed(o, r):
                pool.wait_ge(sem("od_ready"), o * 2 + 2)
                if not (isinstance(o, int) and o < 2):
                    pool.wait_ge(sem("osq_ready"), o - 1)
                    pool.wait_ge(sem("on_ready"), o - 1)
                g.tensor_tensor(om[r], od[r], eg[r], ALU.add).then_inc(sem("mixed_ready"), 1)

            def iteration(i, r):
                if runs(i, -1):
                    blocks(i + 1)
                if runs(i, 0):
                    gates(i, r)
                if runs(i, 1):
                    mixed(i - 1, 1 - r)
            pool.wait_ge(sem("tt_ready"), SG)
            blocks(0)
            for i in range(4):
                iteration(i, i % 2)
            with pool.Fori(2, NO // 2 - 1) as j:
                iteration(j * 2, 0)
                iteration(j * 2 + 1, 1)
            for i in range(NO - 2, NO + 1):
                iteration(i, i % 2)
            ffn_moves(1)

        @block.tensor
        def _(pe):
            mm = nc.tensor.matmul
            tr = nc.tensor.transpose

            def turn_weights():
                pe.wait_ge(consts, 1)
                for n in range(NWT):
                    pe.wait_ge(w_scaled, min(n + 1, 3 * KT))
                    src = wsc[n] if n < 3 * KT else (graw[:, n - 3 * KT, :] if n < NWT - 1 else woraw)
                    if n >= 4:
                        pe.wait_ge(w_taken, n - 3)
                    tr(ps[n % 4][:, 0:P], src, ident[:, :]).then_inc(w_turned, 1)

            def turn_group(s, g, r):
                pe.wait_ge(s["xn_ready"], g * TG + TG)
                if not (isinstance(g, int) and g < 2):
                    pe.wait_ge(s["xnT_taken"], g - 1)
                for k in range(TG):
                    last = tr(ps[4 + 2 * r][:, P * k:P * k + P], XN[:, r, k, :], ident[:, :])
                last.then_inc(s["xn_turned"], 1)

            def ffn(k):
                s = ffn_sems(k)
                pe.wait_ge(fw_in, 16 * 5 * (k + 1))
                pe.wait_ge(consts, k + 1)

                def logits(g):
                    pe.wait_ge(s["xnT_taken"], g + 1)
                    bank = ps[5 + 2 * (g * TG // HN)]
                    for j in range(TG):
                        c = (g * TG + j) % HN * E
                        last = mm(bank[:, c:c + E], YT[:, g % 2, j, :], fc[k].wr, start=True, stop=True)
                    last.then_inc(s["logits_done"], 1)

                def ranks(h):
                    pe.wait_ge(s["onehot_ready"], h + 1)
                    ohh = oh[:, h * HN:(h + 1) * HN, :].rearrange("p t e -> p (t e)")
                    mm(ps[2 * h][:, 0:HN * E], fc[k].tri, ohh, start=True, stop=True)
                    mm(ps[2 * h + 1][:, 0:HN * E], fc[k].onesb, ohh, start=True, stop=True).then_inc(s["ranks_done"], 1)
                turn_group(s, 0, 0)
                for g in range(NG):
                    if g + 1 < NG:
                        turn_group(s, g + 1, (g + 1) % 2)
                    logits(g)
                    if g == NG // 2:
                        ranks(0)
                ranks(1)

                if k == 0:
                    pe.wait_ge(s["rows_ready"], HN + 1)
                    turn_weights()
                    pe.wait_ge(w_taken, NWT)

                def turn_rows(j, r):
                    pe.wait_ge(s["rows_in"][r], j * 16 + 16)
                    for c in range(4):
                        last = tr(ps[r][:, P * c:P * c + P], XE[:, r, c, :], ident[:, :])
                    last.then_inc(s["rows_used"], 1)

                def first_layer(j, r):
                    pe.wait_ge(s["w1_in"][r], j * 16 + 16)
                    pe.wait_ge(s["rowsT_ready"], j * 2 + r + 1)
                    mm(ps[2 + r][:, :], W1[:, r, :], XET[:, r, :], start=True, stop=True).then_inc(s["w1_used"], 1)

                def second_layer(j, r):
                    e = j * 2 + r
                    pe.wait_ge(s["hidden_ready"], e + 1)
                    if not (isinstance(j, int) and j < 1):
                        pe.wait_ge(s["eout_ready"], e - 1)
                    for c in range(4):
                        last = mm(ps[4 + r][:, P * c:P * c + P], HT[:, r, P * c:P * c + P],
                                  fc[k].W2[:, ds(e, 1), :].rearrange("p e d -> p (e d)"),
                                  start=True, stop=True)
                    last.then_inc(s["eout_done"], 1)

                def experts(j, last=False):
                    turn_rows(j, 1)
                    second_layer(j, 0)
                    first_layer(j, 1)
                    if not last:
                        turn_rows(j + 1, 0)
                    second_layer(j, 1)
                    if not last:
                        first_layer(j + 1, 0)
                turn_rows(0, 0)
                first_layer(0, 0)
                experts(0)
                with pe.Fori(1, E // 2 - 1) as j:
                    experts(j)
                experts(E // 2 - 1, True)

            ffn(0)

            def bank_taken(s, n):
                if n < 6:
                    pe.wait_ge(sem("silu_ready"), 6 * s + n + 1)
                elif n < 8:
                    pe.wait_ge(sem("gates_ready"), 8 * s + 2 * (n - 6) + 2)
                else:
                    pe.wait_ge(sem("gates_ready"), 8 * s + 5 + n - 8)

            def project(s, first, part):
                for n in part:
                    kind, b = n // 2, n % 2
                    if n >= 4:
                        bank_taken(s, n - 4)
                    elif not first:
                        bank_taken(s - 1, n + NP - 4)
                    if kind < 3:
                        for j in range(KT):
                            last = mm(ps[n % 4][:, :], cw[:, kind * KT + j, :], XNT[:, b, ds(s * 512 + j, 512)],
                                      start=j == 0, stop=j == KT - 1)
                    else:
                        last = mm(ps[n % 4][:, :], gw[:, kind - 3, :], XNT[:, b, ds(s * 512 + KT - 1, 512)],
                                  start=True, stop=True)
                    last.then_inc(sem("proj_done"), 1)
            hs = [slice(CH * h, CH * h + CH) for h in range(H)]

            def passed():
                pe.sem_inc(sem("pe_passed"), 1)

            def gram(s, first):
                pe.wait_ge(sem("kq_ready"), 2 * s + 2)
                for m in range(M):
                    if m % 8 == 0:
                        if not first:
                            pe.wait_ge(sem("gram_taken"), 4 * s + m // 8 - 3)
                        passed()
                    for q in hs:
                        last = mm(ps[4 + m // 8][q, 64 * (m % 8):64 * (m % 8) + 64], KQ[q, m, 0:CH], KQ[q, m, :], start=True, stop=True)
                    if m % 8 == 7:
                        last.then_inc(sem("gram_banks"), 1)

            attn_in = {n: sem(f"{n}_a") for n in ("xn_ready", "xnT_taken", "xn_turned")}
            for n in range(NG):
                turn_group(attn_in, n, n % 2)
                if n == 1:
                    pe.wait_ge(attn_in["xnT_taken"], 2)
                if 1 <= n < 7:
                    project(0, True, [n - 1])
            project(0, True, range(6, NP))
            pe.wait_ge(attn_in["xnT_taken"], NG)
            project(1, False, range(NP))
            gram(0, True)
            with pe.Fori(1, SG - 1) as i:
                project(i + 1, False, range(NP))
                gram(i, False)
            gram(SG - 1, False)

            flat = lambda a: a.rearrange("p h d -> p (h d)")
            bank = ((2, 3), (6, 7))
            past = lambda o, n: not (isinstance(o, int) and o < n)
            moving = lambda o, c, a0, a1: VKA[:, ds(o * 8 + c, 1), a0:a1].rearrange("p m c -> p (m c)")

            def wu(o, cs):
                for c in cs:
                    if c == 0:
                        pe.wait_ge(sem("bdt_ready"), o + 1)
                        if past(o, 1):
                            pe.wait_ge(sem("bdu_ready"), o * 4)
                            pe.wait_ge(sem("bdw_ready"), o * 4)
                    last = mm(ps[0][:, 64 * c:64 * c + 64], flat(BDT[:, c]), moving(o, c, 0, 64), start=True, stop=True)
                if c == 7:
                    last.then_inc(sem("wu_done"), 1)

            def mq(o, r, cs):
                for c in cs:
                    if c == 0:
                        pe.wait_ge(sem("bdw_ready"), o * 4 + 4)
                        if past(o, 1):
                            pe.wait_ge(sem("p_ready"), o)
                            pe.wait_ge(sem("q_ready"), o)
                    last = mm(ps[1][:, 64 * c:64 * c + 64], flat(BDW[r][:, c]), moving(o, c, CH, 96), start=True, stop=True)
                if c == 7:
                    last.then_inc(sem("mq_done"), 1)

            def inputs_part(o, r, k):
                if k == 0:
                    pe.wait_ge(sem("bdu_ready"), o * 4 + 4)
                    if past(o, 2):
                        pe.wait_ge(sem("od_ready"), o * 2 - 2)
                else:
                    pe.wait_ge(sem("change_ready"), (o * 4 + k) * 2)
                for b in range(B):
                    mm(ps[bank[r][b]][:, 64 * k:64 * k + 64], flat(BDU[r][:, 4 * b + k]),
                       moving(o, 4 * b + k, CH, 96), start=True, stop=False)

            def states_part(o, r, k):
                if k == 0:
                    pe.wait_ge(sem("p_ready"), o + 1)
                    pe.wait_ge(sem("q_ready"), o + 1)
                pe.wait_ge(sem("state_ready"), o * 4 + k + 1)
                for b in range(B):
                    last = mm(ps[bank[r][b]][:, 64 * k:64 * k + 64], flat(BDS[k % 2][:, b]),
                              PQs[r][:, 4 * b + k, :], start=False, stop=True)
                last.then_inc(sem("chain_done"), 1)

            def norms(o, r):
                pe.wait_ge(sem("osq_ready"), o + 1)
                if past(o, 1):
                    pe.wait_ge(sem("ors_ready"), o)
                mm(ps[4][:, 0:256], flat(bdm[:, :, :]), osq[r], start=True, stop=True).then_inc(sem("oss_done"), 1)

            def proj_out(o, r):
                pe.wait_ge(sem("on_ready"), o + 1)
                if past(o, 1):
                    pe.wait_ge(sem("attn_added"), o)
                for b in range(B):
                    last = mm(ps[5][:, P * b:P * b + P], on[r][:, P * b:P * b + P], wo[:, :], start=True, stop=True)
                last.then_inc(sem("wo_done"), 1)

            def other(i, r, n0, n1):
                if runs(i, 0) and 0 <= n0 < 8:
                    mq(i, r, range(n0, min(n1, 8)))
                if runs(i, -1) and n1 > 8:
                    wu(i + 1, range(max(n0, 8) - 8, n1 - 8))

            def iteration(i, r):
                for k in range(4):
                    if runs(i, 1):
                        inputs_part(i - 1, 1 - r, k)
                    other(i, r, 4 * k - 1, 4 * k)
                    if runs(i, 1):
                        states_part(i - 1, 1 - r, k)
                    other(i, r, 4 * k, 4 * k + 3)
                other(i, r, 15, 16)
                if runs(i, 2):
                    norms(i - 2, r)
                if runs(i, 3):
                    proj_out(i - 3, 1 - r)

            def hold_clock(n):
                for _ in range(n):
                    mm(ps[5][:, :], cw[:, 0, :], cw[:, 0:4, :].rearrange("p n d -> p (n d)"), start=True, stop=True)

            pe.wait_ge(sem("tt_ready"), SG)
            pe.wait_ge(sem("a_masked"), SG)
            hold_clock(4)
            wu(0, range(8))
            hold_clock(4)
            iteration(0, 0)
            hold_clock(4)
            iteration(1, 1)
            hold_clock(2)
            iteration(2, 0)
            iteration(3, 1)
            with pe.Fori(2, NO // 2 - 1) as j:
                iteration(j * 2, 0)
                iteration(j * 2 + 1, 1)
            for i in range(NO - 2, NO + 3):
                iteration(i, i % 2)
            ffn(1)

        @block.scalar
        def _(act):
            a = nc.scalar.activation

            def take_weights():
                for n in range(NWT):
                    act.wait_ge(w_turned, n + 1)
                    if n < 3 * KT:
                        a(cw[:, n, :], ps[n % 4][:, 0:P], ACT.Copy).then_inc(w_taken, 1)
                    elif n < NWT - 1:
                        a(gw[:, n - 3 * KT, :], ps[n % 4][:, 0:P], ACT.Copy).then_inc(w_taken, 1)
                    else:
                        act.wait_ge(w_in, 16 * (6 + 3 * H + 1 + 2 * H))
                        a(wo[:, :], ps[n % 4][:, 0:P], ACT.Identity, scale=onw[:, 0:1]).then_inc(w_taken, 1)

            def root(n, c, count):
                act.wait_ge(sem(f"var_ready{n}"), count)
                a(rstd[:, c], var[:, c], ACT.Sqrt, bias=ceps[:, 0:1]).then_inc(sem(f"std_ready{n}"), 1)

            def ffn(k):
                s = ffn_sems(k)
                act.wait_ge(consts, k + 1)
                if k == 0:
                    root(0, slice(0, HN), 1)
                    root(0, slice(HN, NT), 2)
                else:
                    root(1, slice(0, NT), 1)
                for g in range(NG):
                    act.wait_ge(s["xn_turned"], g + 1)
                    if g >= 2:
                        act.wait_ge(s["logits_done"], g - 1)
                    a(YT[:, g % 2].rearrange("p t d -> p (t d)"), ps[4 + 2 * (g % 2)][:, :], ACT.Copy).then_inc(s["xnT_taken"], 1)
                    if g == NG // 2 + 1 or g == NG - 1:
                        h = int(g == NG - 1)
                        exh = ex[:, h * HN:(h + 1) * HN, :]
                        act.wait_ge(s["z_ready"], h + 1)
                        a(exh, exh, ACT.Exp).then_inc(s["exp_ready"], 1)
                if k == 0:
                    take_weights()

                def expert(j, r):
                    e = j * 2 + r
                    act.wait_ge(s["rows_used"], e + 1)
                    a(XET[:, r, :], ps[r][:, :], ACT.Copy).then_inc(s["rowsT_ready"], 1)
                    act.wait_ge(s["w1_used"], e + 1)
                    if not isinstance(j, int):
                        act.wait_ge(s["eout_done"], e - 1)
                    a(HT[:, r, :], ps[2 + r][:, :], ACT.Relu, bias=fc[k].B1[:, ds(e, 1)]).then_inc(s["hidden_ready"], 1)
                expert(0, 0)
                expert(0, 1)
                with act.Fori(1, E // 2) as j:
                    for r in range(2):
                        expert(j, r)

            ffn(0)

            def take(s, first, part):
                for n in part:
                    kind, b = n // 2, n % 2
                    act.wait_ge(sem("proj_done"), s * 12 + n + 1)
                    if not first:
                        if n == 0:
                            act.wait_ge(sem("qk_chunked"), 2 * s - 1)
                        if n == 2:
                            act.wait_ge(sem("qk_chunked"), 2 * s)
                        if n == 4:
                            act.wait_ge(sem("v_chunked"), s)
                            act.wait_ge(sem("gv_ready"), s)
                        if n == 6:
                            act.wait_ge(sem("average_steps"), 2 * s)
                        if n == 8:
                            act.wait_ge(sem("beta_chunked"), s)
                    src = ps[n % 4][:, :]
                    if kind < 3:
                        a((qT, kT, vT)[kind][:, b, :], src, ACT.Silu).then_inc(sem("silu_ready"), 1)
                    elif kind == 3:
                        a(ga[:, b, :], src, ACT.Sigmoid).then_inc(sem("gates_ready"), 1)
                        a(gb[:, b, :], src, ACT.Sigmoid, scale=-1.0).then_inc(sem("gates_ready"), 1)
                    elif kind == 4:
                        a(be[:, b, :], src, ACT.Sigmoid).then_inc(sem("gates_ready"), 1)
                    else:
                        a(MX[:, b, ds(s * 512, 512)], src, ACT.Sigmoid, bias=mbias[:, 0:1]).then_inc(sem("gates_ready"), 1)

            def copy_qk(s):
                for n in range(M // 8):
                    act.wait_ge(sem("gram_banks"), 4 * s + n + 1)
                    a(VKA[:, ds(s * M + 8 * n, 8), 64:96], chunks(ps[4 + n][:, :], 64)[:, :, CH:64],
                      ACT.Copy).then_inc(sem("a_copied"), 1)

            def roots(s):
                act.wait_ge(sem("qk_chunked"), 2 * s + 1)
                a(sqq, qC, ACT.Square).then_inc(sem("sq_ready"), 1)
                act.wait_ge(sem("qk_chunked"), 2 * s + 2)
                a(sqk, kC, ACT.Square).then_inc(sem("sq_ready"), 1)
                act.wait_ge(sem("sums_ready"), 2 * s + 2)
                a(rn[:, :, :], rn[:, :, :], ACT.Sqrt, bias=ceps[:, 2:3]).then_inc(sem("root_ready"), 1)

            def take_turned(n):
                act.wait_ge(sem("xn_turned_a"), n + 1)
                b, l = turns[n] // (NG // B), turns[n] % (NG // B)
                a(XNT[:, b, l * 512 + KT - 1:(l + 1) * 512 + KT - 1], ps[4 + 2 * (n % 2)][:, :], ACT.Copy).then_inc(sem("xnT_taken_a"), 1)

            for n, grp in enumerate(turns):
                act.wait_ge(sem("var_ready_a"), n * TG + TG)
                t4 = slice(grp * TG, grp * TG + TG)
                a(rstd[:, t4], mv[:, t4, 1], ACT.Sqrt, bias=ceps[:, 0:1]).then_inc(sem("std_ready_a"), 1)
                if n >= 1:
                    take_turned(n - 1)
                if n >= 3:
                    take(0, True, [n - 3])
            take_turned(NG - 1)
            take(0, True, range(NG - 3, 12))
            roots(0)
            with act.Fori(1, SG) as i:
                take(i, False, range(12))
                roots(i)
                copy_qk(i - 1)
            copy_qk(SG - 1)

            act.wait_ge(sem("uw_cleared"), 4)

            def spread_w(o, r):
                act.wait_ge(sem("wu_done"), o + 1)
                if not (isinstance(o, int) and o < 2):
                    act.wait_ge(sem("mq_done"), o - 1)
                for h in range(H):
                    q = slice(CH * h, CH * h + CH)
                    a(BDW[r][q, :, h, :], chunks(ps[0][q, :], 64)[:, :, CH:64], ACT.Copy).then_inc(sem("bdw_ready"), 1)

            def spread_u(o, r):
                if not (isinstance(o, int) and o < 2):
                    act.wait_ge(sem("chain_done"), o * 4 - 4)
                for h in range(H):
                    q = slice(CH * h, CH * h + CH)
                    a(BDU[r][q, :, h, :], chunks(ps[0][q, :], 64)[:, :, 0:CH], ACT.Copy).then_inc(sem("bdu_ready"), 1)

            def take_p(o, r):
                act.wait_ge(sem("mq_done"), o + 1)
                if not (isinstance(o, int) and o < 2):
                    act.wait_ge(sem("chain_done"), o * 4 - 4)
                a(PQs[r][:, :, 0:CH], chunks(ps[1][:, :], 64)[:, :, 0:CH], ACT.Copy, scale=-1.0).then_inc(sem("p_ready"), 1)

            def square(o, r):
                act.wait_ge(sem("mixed_ready"), o + 1)
                if not (isinstance(o, int) and o < 2):
                    act.wait_ge(sem("oss_done"), o - 1)
                a(osq[r], om[r], ACT.Square).then_inc(sem("osq_ready"), 1)

            def rms(o, r):
                act.wait_ge(sem("oss_done"), o + 1)
                if not (isinstance(o, int) and o < 2):
                    act.wait_ge(sem("on_ready"), o - 1)
                a(ors[r], ps[4][:, 0:256], ACT.Sqrt, bias=ceps[:, 1:2], scale=1.0 / CH).then_inc(sem("ors_ready"), 1)

            def iteration(i, r):
                if runs(i, 0):
                    spread_w(i, r)
                if runs(i, 3):
                    rms(i - 3, 1 - r)
                if runs(i, 2):
                    square(i - 2, r)
                if runs(i, 0):
                    spread_u(i, r)
                    take_p(i, r)
            for i in range(6):
                iteration(i, i % 2)
            with act.Fori(3, NO // 2) as j:
                iteration(j * 2, 0)
                iteration(j * 2 + 1, 1)
            for i in range(NO, NO + 3):
                iteration(i, i % 2)
            ffn(1)

        @block.vector
        def _(dve):
            v = nc.vector
            dve_steps = Steps(dve, sem("dve_steps"))
            did = dve_steps.did

            did(v.memset(XG[:, :, :], 0.0))
            dve_steps.wait()
            dve.sem_inc(zero_ready, 1)

            def scale_weights():
                dve.wait_ge(w_in, 16 * (6 + 3 * H + 1 + 2 * H))
                for n in range(3 * KT):
                    v.tensor_scalar(wsc[n], wraw[:, n // KT, :], craw[:, n // KT, n % KT:n % KT + 1], None, ALU.mult).then_inc(w_scaled, 1)

            def first_stats(h):
                for q in range(h * XQ // 2, (h + 1) * XQ // 2):
                    dve.wait_ge(sem(f"x_in_{q}"), 16)
                    for t1 in range(q * NT // XQ, (q + 1) * NT // XQ):
                        did(v.bn_stats(st[:, t1, :], X[:, t1, :]))
                dve_steps.wait()

            def means(n, c):
                did(v.tensor_tensor(mean[:, c], st[:, c, 1], st[:, c, 4], ALU.subtract))
                did(v.tensor_tensor(var[:, c], st[:, c, 2], st[:, c, 5], ALU.add))
                dve_steps.wait()
                did(v.scalar_tensor_tensor(out=rstd[:, c], in0=mean[:, c], scalar=0.25, in1=mean[:, c], op0=ALU.mult, op1=ALU.mult))
                dve_steps.wait()
                did(v.tensor_tensor(mean[:, c], st[:, c, 1], st[:, c, 4], ALU.add))
                dve_steps.wait()
                v.scalar_tensor_tensor(out=var[:, c], in0=var[:, c], scalar=1.0 / D, in1=rstd[:, c], op0=ALU.mult,
                                       op1=ALU.add).then_inc(sem(f"var_ready{n}"), 1)
                did(v.tensor_scalar(mean[:, c], mean[:, c], 0.5, None, ALU.mult))
                dve_steps.wait()

            def invert(n, c, count):
                dve.wait_ge(sem(f"std_ready{n}"), count)
                did(v.reciprocal(rstd[:, c], rstd[:, c]))
                dve_steps.wait()

            def normalise(n, g):
                r = g % 2
                if g >= 2:
                    dve.wait_ge(sem(f"xn_turned{n}"), g - 1)
                for k in range(TG):
                    t1 = g * TG + k
                    v.tensor_scalar(XN[:, r, k, :], X[:, t1, :], mean[:, t1:t1 + 1], rstd[:, t1:t1 + 1],
                                    ALU.subtract, ALU.mult).then_inc(sem(f"xn_ready{n}"), 1)

            def ffn(k):
                s = ffn_sems(k)
                T = [slice(h * HN, (h + 1) * HN) for h in range(2)]
                if k == 0:
                    first_stats(0)
                    means(0, T[0])
                    invert(0, T[0], 1)
                    normalise(0, 0)
                    normalise(0, 1)
                    first_stats(1)
                    means(0, T[1])
                    invert(0, T[1], 2)
                else:
                    means(1, slice(0, NT))
                    invert(1, slice(0, NT), 1)
                    normalise(1, 0)
                    normalise(1, 1)
                bce = lambda a: a.unsqueeze(2).to_broadcast([P, HN, E])
                bct = lambda a: a.unsqueeze(1).to_broadcast([P, HN, E])

                def choose(h):
                    lgh, exh, eqh = lg[:, T[h], :], ex[:, T[h], :], eq[:, T[h], :]
                    dve.wait_ge(s["logits_done"], (h + 1) * NG // 2)
                    did(v.tensor_tensor(lgh, by_tile(ps[5 + 2 * h][:, 0:HN * E]), bct(fc[k].brb), ALU.add))
                    dve_steps.wait()
                    did(v.tensor_reduce(mx[:, T[h]], lgh, AX_X, ALU.max))
                    dve_steps.wait()
                    v.tensor_tensor(exh, lgh, bce(mx[:, T[h]]), ALU.subtract).then_inc(s["z_ready"], 1)
                    did(v.tensor_tensor(eqh, lgh, bce(mx[:, T[h]]), ALU.is_equal))
                    dve_steps.wait()
                    did(v.tensor_tensor(eqh, eqh, bct(fc[k].rev), ALU.mult))
                    dve_steps.wait()
                    did(v.tensor_reduce(mrev[:, T[h]], eqh, AX_X, ALU.max))
                    dve_steps.wait()
                    v.tensor_tensor(oh[:, T[h], :], bct(fc[k].rev), bce(mrev[:, T[h]]), ALU.is_equal).then_inc(s["onehot_ready"], 1)

                def place(h):
                    toth, inclh, cumh = half(tot, h), half(incl, h), cum[:, T[h], :]
                    gateh, keeph, sloth, tmph, trashh = gate[:, T[h]], keep[:, T[h]], slot[:, T[h]], tmp1[:, T[h]], fc[k].trash[:, T[h]]
                    dve.wait_ge(s["exp_ready"], h + 1)
                    did(v.tensor_reduce(sm[:, T[h]], ex[:, T[h], :], AX_X, ALU.add))
                    dve.wait_ge(s["ranks_done"], h + 1)
                    did(v.tensor_copy(eview(toth), by_tile(ps[2 * h + 1][:, 0:HN * E])))
                    dve_steps.wait(1)
                    did(v.reciprocal(gateh, sm[:, T[h]]))
                    dve_steps.wait(1)
                    did(v.tensor_tensor_scan(inclh, half(fc[k].rmask, h), toth, 0.0, ALU.mult, ALU.add))
                    dve_steps.wait()
                    did(v.tensor_tensor(toth, inclh, toth, ALU.subtract))
                    dve_steps.wait()
                    did(v.tensor_tensor(toth, toth, half(fc[k].eoff, h), ALU.add))
                    dve_steps.wait()
                    if h:
                        did(v.tensor_tensor(by_expert(toth), by_expert(toth),
                                            by_expert(half(incl, 0))[:, :, HN - 1:HN].to_broadcast([P, E, HN]), ALU.add))
                        dve_steps.wait()
                    did(v.tensor_tensor(cumh, by_tile(ps[2 * h][:, 0:HN * E]), eview(toth), ALU.add))
                    dve_steps.wait()
                    did(v.tensor_tensor(cumh, cumh, oh[:, T[h], :], ALU.mult))
                    dve_steps.wait()
                    did(v.tensor_reduce(sloth, cumh, AX_X, ALU.add))
                    dve_steps.wait()
                    did(v.scalar_tensor_tensor(out=tmph, in0=mrev[:, T[h]], scalar=float(CAP), in1=sloth, op0=ALU.mult, op1=ALU.add))
                    dve_steps.wait()
                    did(v.tensor_scalar(keeph, tmph, float(CAP * E + CAP), None, ALU.is_lt))
                    dve_steps.wait()
                    did(v.tensor_tensor(gateh, gateh, keeph, ALU.mult))
                    did(v.tensor_tensor(gidx[:, T[h]], sloth, keeph, ALU.mult))
                    did(v.tensor_tensor(tmph, sloth, trashh, ALU.subtract))
                    dve_steps.wait()
                    did(v.tensor_tensor(tmph, tmph, keeph, ALU.mult))
                    did(v.tensor_scalar(hgate[:, T[h]], gateh, 0.5, None, ALU.mult))
                    did(v.tensor_tensor(rstd[:, T[h]], rstd[:, T[h]], gateh, ALU.mult))
                    dve_steps.wait()
                    did(v.tensor_tensor(sidx[:, T[h]], tmph, trashh, ALU.add))
                    dve_steps.wait()

                def rows(h):
                    with dve.Fori(h * NG // 2, (h + 1) * NG // 2) as g:
                        for j in range(TG):
                            t1 = g * TG + j
                            v.tensor_scalar(XG[:, ds(t1, 1), :].rearrange("p t d -> p (t d)"),
                                            X[:, ds(t1, 1), :].rearrange("p t d -> p (t d)"),
                                            mean[:, ds(t1, 1)], rstd[:, ds(t1, 1)], ALU.subtract, ALU.mult).then_inc(s["rows_ready"], 1)
                for g in range(2, NG // 2 + 2):
                    normalise(k, g)
                dve.wait_ge(fw_in, 16 * 5 * (k + 1))
                dve.wait_ge(consts, k + 1)
                choose(0)
                for g in range(NG // 2 + 2, NG - 1):
                    normalise(k, g)
                place(0)
                normalise(k, NG - 1)
                if k == 0:
                    dve.wait_ge(zeroed, 16 * E)
                rows(0)
                choose(1)
                place(1)
                rows(1)

                if k == 0:
                    scale_weights()

                def expert(j, r):
                    e = j * 2 + r
                    dve.wait_ge(s["eout_done"], e + 1)
                    if not isinstance(j, int):
                        dve.wait_ge(s["stored"][r], j * 16)
                    v.tensor_tensor(EO[:, r], ps[4 + r][:, :].rearrange("p (s d) -> p s d", s=4),
                                    fc[k].B2[:, ds(e, 1), :].to_broadcast([P, 4, D]), ALU.add).then_inc(s["eout_ready"], 1)
                expert(0, 0)
                expert(0, 1)
                with dve.Fori(1, E // 2) as j:
                    for r in range(2):
                        expert(j, r)

                def gathered(grp):
                    dve.wait_ge(sem(f"gathered{k}_{grp}"), 16 * TG)
                    for m in range(grp * TG, grp * TG + TG):
                        v.scalar_tensor_tensor(out=X[:, m, :], in0=XG[:, m, :], scalar=hgate[:, m:m + 1], in1=X[:, m, :],
                                               op0=ALU.mult, op1=ALU.add).then_inc(sem(f"added{k}"), 1)
                if k:
                    for n in range(NG):
                        gathered(n)
                    return

                def stats(n, grp):
                    dve.wait_ge(sem("added0"), n * TG + TG)
                    for m in range(grp * TG, grp * TG + TG):
                        did(v.bn_stats(st[:, m, :], X[:, m, :]))
                    dve_steps.wait()
                    for m in range(grp * TG, grp * TG + TG):
                        v.bn_aggr(mv[:, m, :], st[:, m, :]).then_inc(sem("var_ready_a"), 1)

                def normalise_group(n, grp):
                    dve.wait_ge(sem("std_ready_a"), n + 1)
                    t4 = slice(grp * TG, grp * TG + TG)
                    did(v.reciprocal(rstd[:, t4], rstd[:, t4]))
                    dve_steps.wait()
                    if n >= 2:
                        dve.wait_ge(sem("xn_turned_a"), n - 1)
                    for j in range(TG):
                        m = grp * TG + j
                        v.tensor_scalar(XN[:, n % 2, j, :], X[:, m, :], mv[:, m, 0:1], rstd[:, m:m + 1],
                                        ALU.subtract, ALU.mult).then_inc(sem("xn_ready_a"), 1)
                for n, grp in enumerate(turns):
                    gathered(grp)
                    stats(n, grp)
                    if n >= 1:
                        normalise_group(n - 1, turns[n - 1])
                normalise_group(NG - 1, turns[NG - 1])

            ffn(0)

            turned = lambda a: a.rearrange("p b (q x) -> p q b x", x=P)
            row = lambda a: a.rearrange("p m d -> p (m d)")

            def front(s, first):
                if not first:
                    dve.wait_ge(sem("qn_kept"), s)
                dve.wait_ge(sem("silu_ready"), 6 * s + 2)
                v.transpose(row(qC), turned(qT)).then_inc(sem("qk_chunked"), 1)
                dve.wait_ge(sem("silu_ready"), 6 * s + 4)
                v.transpose(row(kC), turned(kT)).then_inc(sem("qk_chunked"), 1)
                dve.wait_ge(sem("silu_ready"), 6 * s + 6)
                v.transpose(row(vC), turned(vT)).then_inc(sem("v_chunked"), 1)
                dve.wait_ge(sem("gates_ready"), 8 * s + 6)
                v.transpose(row(bC), turned(be)).then_inc(sem("beta_chunked"), 1)
                dve.wait_ge(sem("sq_ready"), 2 * s + 1)
                v.tensor_reduce(rn[:, 0, :], sqq, AX_X, ALU.add).then_inc(sem("sums_ready"), 1)
                dve.wait_ge(sem("sq_ready"), 2 * s + 2)
                v.tensor_reduce(rn[:, 1, :], sqk, AX_X, ALU.add).then_inc(sem("sums_ready"), 1)
                dve.wait_ge(sem("beta_chunked"), s + 1)
                v.tensor_scalar(nbeta[:, ds(s * M, M)], bC[:, :, 0], -1.0, None, ALU.mult).then_inc(sem("beta_kept"), 1)
                v.tensor_copy(beta[:, ds(s * M, M)], bC[:, :, 0]).then_inc(sem("beta_kept"), 1)
                dve.wait_ge(sem("gv_ready"), s + 1)
                if not first:
                    dve.wait_ge(sem("average_steps"), 2 * s)
                for b in range(B):
                    v.tensor_tensor_scan(EM[:, b, ds(s * 512, 512)], ga[:, b, :], gb[:, b, :],
                                         0.0 if first else EM[:, b, ds(s * 512 - 1, 1)], ALU.mult, ALU.add).then_inc(sem("average_steps"), 1)
                dve.wait_ge(sem("root_ready"), s + 1)
                v.reciprocal(rn[:, :, :], rn[:, :, :]).then_inc(sem("norms_ready"), 1)
                dve.wait_ge(sem("norms_ready"), s + 1)
                did(v.tensor_tensor(qC, qC, rn[:, 0, :].unsqueeze(2).to_broadcast([P, M, CH]), ALU.mult))
                dve_steps.wait()
                if not first:
                    dve.wait_ge(sem("gram_banks"), 4 * s)
                v.transpose(KQ[:, :, CH:64], qC).then_inc(sem("kq_ready"), 1)
                dve.wait_ge(sem("k_normed"), s + 1)
                v.transpose(KQ[:, :, 0:CH], kC).then_inc(sem("kq_ready"), 1)

            def solve(s, fronts):
                dve.wait_ge(sem("kq_ready"), 2 * fronts)
                dve.wait_ge(sem("beta_kept"), 2 * fronts)
                for n in range(M // 8):
                    dve.wait_ge(sem("a_copied"), 4 * s + n + 1)
                    pv = ps[4 + n][:, :].rearrange("p (c x) -> p c x", x=64)
                    v.tensor_tensor(AG[:, 8 * n:8 * n + 8, :], pv[:, :, 0:CH],
                                    nbeta[:, ds(s * M + 8 * n, 8)].unsqueeze(2).to_broadcast([P, 8, CH]), ALU.mult).then_inc(sem("gram_taken"), 1)
                dve.wait_ge(sem("gram_taken"), 4 * s + 4)
                did(v.transpose(RA, AG.rearrange("p m j -> p j m")))
                dve_steps.wait()
                dve.wait_ge(sem("rt_ready"), s + 1)
                for j in range(CH - 1):
                    n = CH - 1 - j
                    cuts = [(j + 1, CH)] if n < 3 else [(j + 1, j + 1 + (n + 1) // 2), (j + 1 + (n + 1) // 2, CH)]
                    back = len(cuts) - 1
                    w = j + 1
                    parts = []
                    for lo, hi in cuts:
                        pr = prod[j % 2][:, (lo - j - 1) * w:(hi - j - 1) * w].rearrange("p (i c) -> p i c", c=w)
                        did(v.tensor_tensor(pr, RA[:, j, lo:hi].unsqueeze(2).to_broadcast([P, hi - lo, w]),
                                            RT[:, j:j + 1, 0:w].to_broadcast([P, hi - lo, w]), ALU.mult))
                        parts.append((lo, hi, pr))
                    for lo, hi, pr in parts:
                        dve_steps.wait(back)
                        did(v.tensor_tensor(RT[:, lo:hi, 0:w], RT[:, lo:hi, 0:w], pr, ALU.add))
                    dve_steps.wait(back)
                dve_steps.wait()
                did(v.transpose(TC.rearrange("p m i -> p i m"), RT))
                dve_steps.wait()
                v.tensor_tensor(TT[:, ds(s * 1024, 1024)].rearrange("p (m d) -> p m d", d=CH), TC,
                                beta[:, ds(s * M, M)].unsqueeze(2).to_broadcast([P, M, CH]), ALU.mult).then_inc(sem("tt_ready"), 1)
                dve.wait_ge(sem("tt_ready"), s + 1)

            split = sum(2 if CH - 1 - j < 3 else 4 for j in range(CH - 1))
            front(0, True)
            with dve.Fori(0, SG - 1) as i:
                dve_steps.enter(i, 0, 1 + 1 + split + 1)
                front(i + 1, False)
                solve(i, i + 2)
            dve_steps.leave(SG - 1)
            dve.wait_ge(sem("qn_kept"), SG)
            solve(SG - 1, SG)

            v.memset(BDU[0], 0.0).then_inc(sem("uw_cleared"), 1)
            v.memset(BDW[0], 0.0).then_inc(sem("uw_cleared"), 1)
            v.memset(Sc, 0.0).then_inc(sem("s_ready"), 1)
            v.memset(BDS[0], 0.0).then_inc(sem("state_ready"), 1)
            v.memset(BDU[1], 0.0).then_inc(sem("uw_cleared"), 1)
            v.memset(BDW[1], 0.0).then_inc(sem("uw_cleared"), 1)

            bank = ((2, 3), (6, 7))

            def next_state(o, r, k):
                n = o * 4 + k + 1
                dve.wait_ge(sem("chain_done"), n)
                dve.wait_ge(sem("s_ready"), n)
                for b in range(B):
                    v.transpose(dT[:, CH * b:CH * b + CH], ps[bank[r][b]][:, 64 * k:64 * k + CH]).then_inc(sem("change_ready"), 1)
                dve.wait_ge(sem("change_ready"), n * 2)
                v.tensor_tensor(Sc, Sc, dT, ALU.add).then_inc(sem("s_ready"), 1)
                dve.wait_ge(sem("s_ready"), n + 1)
                v.tensor_tensor(BDS[(k + 1) % 2], both(Sc).unsqueeze(2).to_broadcast([P, B, H, CH]),
                                bdm[:, :, :].unsqueeze(1).to_broadcast([P, B, H, CH]), ALU.mult).then_inc(sem("state_ready"), 1)

            def take_q(o, r):
                dve.wait_ge(sem("mq_done"), o + 1)
                dve.wait_ge(sem("p_ready"), o + 1)
                v.tensor_tensor(PQs[r][:, :, CH:64], QN[:, ds(o * 8, 8), :], chunks(ps[1][:, :], 64)[:, :, CH:64],
                                ALU.subtract).then_inc(sem("q_ready"), 1)

            def gated_output(o, r):
                dve.wait_ge(sem("chain_done"), o * 4 + 4)
                dve.wait_ge(sem("mixing_ready"), o * 2 + 2)
                if not (isinstance(o, int) and o < 2):
                    dve.wait_ge(sem("mixed_ready"), o - 1)
                for b in range(B):
                    v.tensor_tensor(chunks(both(od[r])[:, b, :]), chunks(ps[bank[r][b]][:, 0:256], 64)[:, :, CH:64],
                                    chunks(both(mi[r])[:, b, :]), ALU.mult).then_inc(sem("od_ready"), 1)

            def invert_rms(o, r, b):
                dve.wait_ge(sem("ors_ready"), o + 1)
                v.reciprocal(both(ors[r])[:, b, :], both(ors[r])[:, b, :]).then_inc(sem("inverse_ready"), 1)

            def scaled(o, r):
                dve.wait_ge(sem("inverse_ready"), o * 2 + 2)
                dve.wait_ge(sem("mixed_ready"), o + 1)
                if not (isinstance(o, int) and o < 2):
                    dve.wait_ge(sem("wo_done"), o - 1)
                v.tensor_tensor(on[r], om[r], ors[r], ALU.mult).then_inc(sem("on_ready"), 1)

            def residual(o):
                dve.wait_ge(sem("wo_done"), o + 1)
                xo = X[:, :, :].rearrange("p (b t) d -> p b t d", b=B)[:, :, ds(o, 1), :].rearrange("p b t d -> p b (t d)")
                v.tensor_tensor(xo, xo, both(ps[5][:, 0:256]), ALU.add).then_inc(sem("attn_added"), 1)

            def next_stats(o):
                dve.wait_ge(sem("attn_added"), o + 1)
                for b in range(B):
                    t1 = o + b * NO
                    v.bn_stats(st[:, ds(t1, 1), :].rearrange("p t x -> p (t x)"),
                               X[:, ds(t1, 1), :].rearrange("p t d -> p (t d)")).then_inc(sem("stats_ready"), 1)

            def iteration(i, r):
                for k in range(4):
                    if runs(i, 1):
                        next_state(i - 1, 1 - r, k)
                    if k == 3 and runs(i, 4):
                        residual(i - 4)
                    if k < 2 and runs(i, 3):
                        invert_rms(i - 3, 1 - r, k)
                    if k == 2:
                        if runs(i, 0):
                            take_q(i, r)
                        if runs(i, 3):
                            scaled(i - 3, 1 - r)
                if runs(i, 1):
                    gated_output(i - 1, 1 - r)
                if runs(i, 4):
                    next_stats(i - 4)
            for i in range(6):
                iteration(i, i % 2)
            with dve.Fori(3, NO // 2) as j:
                iteration(j * 2, 0)
                iteration(j * 2 + 1, 1)
            for i in range(NO, NO + 4):
                iteration(i, i % 2)
            dve.wait_ge(sem("attn_added"), NO)
            dve.wait_ge(sem("stats_ready"), NT)
            dve.sem_inc(sem("attn_done"), 1)
            ffn(1)


_INS = ["L0_attn_hidden_states", "L0_attn_Wq", "L0_attn_Wk", "L0_attn_Wv", "L0_attn_Wb", "L0_attn_Wdec",
        "L0_attn_Wmix", "L0_attn_mix_bias", "L0_attn_wq_conv", "L0_attn_wk_conv", "L0_attn_wv_conv",
        "L0_attn_onorm_w", "L0_attn_Wo", "L0_ffn_Wr", "L0_ffn_br", "L0_ffn_W1", "L0_ffn_b1", "L0_ffn_W2",
        "L0_ffn_b2"]


def kernel(**inputs):
    import numpy as _np
    import concourse.bacc as _bacc
    from concourse import mybir as _mybir
    from concourse.bass_utils import run_bass_kernel_spmd as _run

    nc = _bacc.Bacc("TRN2", target_bir_lowering=False, num_devices=1)
    arrays, tensors = {}, {}
    for name in _INS:
        a = _np.ascontiguousarray(inputs[name])
        arrays[f"in_{name}"] = a
        tensors[name] = nc.dram_tensor(f"in_{name}", a.shape, _mybir.dt.from_np(a.dtype), kind="ExternalInput").ap()
    shape = tuple(inputs["L0_attn_hidden_states"].shape)
    out = nc.dram_tensor("out_x", shape, _mybir.dt.from_np(_np.dtype("float32")), kind="ExternalOutput").ap()
    macaron_kernel(nc, tensors, out)
    r = _run(nc, [arrays], core_ids=[0])
    return r.results[0]["out_x"]
```
